# Optimizing a Trainium2 kernel written in Bass

```python
import numpy as np
import jax
import jax.numpy as jnp

def _softmax(x, axis=-1):
    return jax.nn.softmax(x, axis=axis)

def _gelu(x):
    return jax.nn.gelu(x, approximate=True)

def _silu(x):
    return jax.nn.silu(x)

def _sigmoid(x):
    return jax.nn.sigmoid(x)

def _layernorm(x, axis=-1, eps=1e-05):
    m = jnp.mean(x, axis=axis, keepdims=True)
    v = jnp.var(x, axis=axis, keepdims=True)
    return (x - m) / jnp.sqrt(v + eps)

def _scatter_add(tgt, idx, src, axis=0):
    return tgt.at[idx].add(src)

def _segment_sum(src, seg, n):
    return jax.ops.segment_sum(src, seg, n)
kernel_name = 'mk_sandwich_d1_jaxref_r4_fa2979'

def setup_inputs(seed: int=0):
    np.random.seed(seed)
    _w = jnp.asarray

    def _L0_attn_setup():
        import jax, jax.numpy as jnp
        import numpy as np
        STATE_DIM = 256
        INPUT_DIM = 256
        OUTPUT_DIM = 256
        BATCH = 8
        SEQ = 512
        key = jax.random.key(seed)
        k_x, k_a, k_b, k_w, k_bias = jax.random.split(key, 5)
        x = jax.random.normal(k_x, (BATCH, SEQ, INPUT_DIM), dtype=jnp.float32)
        A = jax.random.uniform(k_a, (STATE_DIM,), dtype=jnp.float32, minval=0.0, maxval=0.99)
        B = jax.random.normal(k_b, (STATE_DIM, INPUT_DIM), dtype=jnp.float32) / np.sqrt(INPUT_DIM)
        W = jax.random.normal(k_w, (OUTPUT_DIM, STATE_DIM), dtype=jnp.float32) / np.sqrt(STATE_DIM)
        b = jax.random.normal(k_bias, (OUTPUT_DIM,), dtype=jnp.float32) * 0.01
        return {'x': x, 'A': A, 'B': B, 'W': W, 'b': b}
    _L0_attn_in = _L0_attn_setup()

    def _L0_ffn_setup():
        import jax, jax.numpy as jnp
        import numpy as np
        D_IN, D_HID = (256, 1024)

        def _ternary(key, shape):
            return jax.random.randint(key, shape, -1, 2).astype(jnp.float32)

        def _tlin(x, w, s):
            return jnp.einsum('bsi,oi->bso', x, w) * s
        key = jax.random.key(seed)
        ks = jax.random.split(key, 12)
        inv = lambda fan: 1.0 / np.sqrt(fan).astype(np.float32)
        return {'x': jax.random.normal(ks[0], (4, 512, D_IN), dtype=jnp.float32), 'w1_w': _ternary(ks[1], (D_HID, D_IN)), 'w1_s': jax.random.uniform(ks[2], (D_HID,), dtype=jnp.float32) * inv(D_IN), 'w2_w': _ternary(ks[3], (D_HID, D_IN)), 'w2_s': jax.random.uniform(ks[4], (D_HID,), dtype=jnp.float32) * inv(D_IN), 'h1_w': _ternary(ks[5], (D_HID, D_HID)), 'h1_s': jax.random.uniform(ks[6], (D_HID,), dtype=jnp.float32) * inv(D_HID), 'h2_w': _ternary(ks[7], (D_HID, D_HID)), 'h2_s': jax.random.uniform(ks[8], (D_HID,), dtype=jnp.float32) * inv(D_HID), 'w3_w': _ternary(ks[9], (D_IN, D_HID)), 'w3_s': jax.random.uniform(ks[10], (D_IN,), dtype=jnp.float32) * inv(D_HID)}
    _L0_ffn_in = _L0_ffn_setup()
    _d = {'L0_attn_x': _L0_attn_in['x'], 'L0_attn_A': _L0_attn_in['A'], 'L0_attn_B': _L0_attn_in['B'], 'L0_attn_W': _L0_attn_in['W'], 'L0_attn_b': _L0_attn_in['b'], 'L0_ffn_w1_w': _L0_ffn_in['w1_w'], 'L0_ffn_w1_s': _L0_ffn_in['w1_s'], 'L0_ffn_w2_w': _L0_ffn_in['w2_w'], 'L0_ffn_w2_s': _L0_ffn_in['w2_s'], 'L0_ffn_h1_w': _L0_ffn_in['h1_w'], 'L0_ffn_h1_s': _L0_ffn_in['h1_s'], 'L0_ffn_h2_w': _L0_ffn_in['h2_w'], 'L0_ffn_h2_s': _L0_ffn_in['h2_s'], 'L0_ffn_w3_w': _L0_ffn_in['w3_w'], 'L0_ffn_w3_s': _L0_ffn_in['w3_s']}
    _x0 = _d['L0_attn_x']
    _d['L0_attn_x'] = jax.random.normal(jax.random.fold_in(jax.random.key(seed), 1), (16, 512, 256), dtype=_x0.dtype)
    del _x0
    return _d

def reference(L0_attn_x, L0_attn_A, L0_attn_B, L0_attn_W, L0_attn_b, L0_ffn_w1_w, L0_ffn_w1_s, L0_ffn_w2_w, L0_ffn_w2_s, L0_ffn_h1_w, L0_ffn_h1_s, L0_ffn_h2_w, L0_ffn_h2_s, L0_ffn_w3_w, L0_ffn_w3_s):

    def _L0_attn_ref(x, A, B, W, b):
        import jax, jax.numpy as jnp
        import numpy as np
        STATE_DIM = 256
        INPUT_DIM = 256
        OUTPUT_DIM = 256
        BATCH = 8
        SEQ = 512
        u = jnp.einsum('bld,nd->bln', x, B)
        aa = jnp.broadcast_to(A, u.shape)

        def combine(c1, c2):
            a1, b1 = c1
            a2, b2 = c2
            return (a1 * a2, a2 * b1 + b2)
        _, h = jax.lax.associative_scan(combine, (aa, u), axis=1)
        return jnp.einsum('bln,on->blo', h, W) + b

    def _L0_ffn_ref(x, w1_w, w1_s, w2_w, w2_s, h1_w, h1_s, h2_w, h2_s, w3_w, w3_s):
        import jax, jax.numpy as jnp
        import numpy as np
        D_IN, D_HID = (256, 1024)

        def _ternary(key, shape):
            return jax.random.randint(key, shape, -1, 2).astype(jnp.float32)

        def _tlin(x, w, s):
            return jnp.einsum('bsi,oi->bso', x, w) * s
        h = jax.nn.silu(_tlin(x, w1_w, w1_s)) * _tlin(x, w2_w, w2_s)
        h = jax.nn.gelu(_tlin(h, h1_w, h1_s), approximate=False)
        h = jax.nn.gelu(_tlin(h, h2_w, h2_s), approximate=False)
        return _tlin(h, w3_w, w3_s)
    x = L0_attn_x
    x = x + _layernorm(_L0_attn_ref(_layernorm(x, axis=-1), L0_attn_A, L0_attn_B, L0_attn_W, L0_attn_b), axis=-1)
    x = x + _layernorm(_L0_ffn_ref(_layernorm(x, axis=-1), L0_ffn_w1_w, L0_ffn_w1_s, L0_ffn_w2_w, L0_ffn_w2_s, L0_ffn_h1_w, L0_ffn_h1_s, L0_ffn_h2_w, L0_ffn_h2_s, L0_ffn_w3_w, L0_ffn_w3_s), axis=-1)
    return x

_drawn_inputs = setup_inputs


def setup_inputs(seed=0):
    import zlib

    import numpy as np

    out = dict(_drawn_inputs(seed))
    spreads = {}
    factors = {'L0_attn_b': 8.0}
    for name, (base, spread) in spreads.items():
        noise = np.random.default_rng([zlib.crc32(name.encode()), seed]).standard_normal(out[name].shape)
        drawn = base * np.exp(spread * noise) if base else spread * noise
        out[name] = jnp.asarray(drawn.astype(out[name].dtype))
    for name, factor in factors.items():
        out[name] = (out[name] * factor).astype(out[name].dtype)
    return out
```

```python
from contextlib import ExitStack

import concourse.bass as bass
from concourse import mybir

P = 128
ALU = mybir.AluOpType
ACT = mybir.ActivationFunctionType
F32 = mybir.dt.float32
F16 = mybir.dt.float16
I32 = mybir.dt.int32
AX_X = mybir.AxisListType.X

EPS = 1e-5
A_X, A_H0, A_H1, A_H2 = 8, 6, 5, 8


class Tile:

    def __init__(self, pair, par):
        self.pair, self.par = pair, par
        self.n = pair * 2 + par

    def next(self):
        return Tile(self.pair, 1) if self.par == 0 else Tile(self.pair + 1, 0)

    def prev(self):
        return Tile(self.pair, 0) if self.par == 1 else Tile(self.pair - 1, 1)


def ssm_ffn_kernel(nc, x, bw, a_cols, w_all, s_cols, rows, out):
    NT, L, D = x.shape
    J = L // P
    KD = D // P
    HID = s_cols.shape[2] * P
    KH = HID // P
    assert NT % 2 == 0 and L == 512 and KD == 2
    PAIRS = NT // 2
    WCOLS = w_all.shape[1]
    W1, W2, H1 = 0, KD * HID, 2 * KD * HID
    H2 = H1 + KH * HID
    W3 = H2 + KH * HID
    assert W3 + KH * D == WCOLS
    WC = 2048
    NWC = WCOLS // WC
    STAGES = (WCOLS // 2) // WC
    PIECES_UP = 2 * KD * HID // WC
    PIECES_H1 = PIECES_UP + KH * HID // WC
    PIECES_H2 = PIECES_H1 + KH * HID // WC

    ctx = ExitStack()
    with ctx:
        def sb(name, shape, dt=F32):
            return ctx.enter_context(nc.sbuf_tensor(name, shape, dt))

        def psum(name):
            return ctx.enter_context(nc.psum_tensor(name, [P, 512], F32))

        def sem(name):
            return ctx.enter_context(nc.semaphore(name))

        w_f32 = sb("w_f32", [P, WCOLS])
        w_f16 = w_f32[:, 0:WCOLS // 2].bitcast(F16)
        bw_sb = sb("bw_sb", [P, 2, KD, D])
        a_sb = sb("a_sb", [P, KD])
        a_wide = sb("a_wide", [P, KD, L])
        s_sb = sb("s_sb", [P, 4, KH])
        tanh_scale = sb("tanh_scale", [P, KH])
        gate_scale = sb("gate_scale", [P, KH])
        ss = sb("ss", [P, KH])
        mix_scale = sb("mix_scale", [P, 2, KH])
        rows_sb = sb("rows_sb", [P, 2, D])
        b_wide = sb("b_wide", [P, 2, D])
        s3_wide = sb("s3_wide", [P, 2, D])
        ident = sb("ident", [P, P])
        eps = sb("eps", [P, J])
        minus_half = sb("minus_half", [P, J])
        var_plus = sb("var_plus", [P, 4, J])
        ones = sb("ones", [P, 1])
        agrees = sb("agrees", [P, WC], F16)
        agreed = sb("agreed", [P, WC], F16)
        bad = sb("bad", [P, J + 1])
        scratch = sb("scratch", [P, 1])
        least = sb("least", [P, 1])
        bad_sum = sb("bad_sum", [P, 1])
        fine = sb("fine", [1, 1], I32)

        x_in = [sb(f"x_in{i}", [P, J, D]) for i in range(2)]
        x_mid = [sb(f"x_mid{i}", [P, J, D]) for i in range(2)]
        x_out = [sb(f"x_out{i}", [P, J, D]) for i in range(2)]
        normed = sb("normed", [P, J, D])
        y_sb = sb("y_sb", [P, J, D])
        z_sb = sb("z_sb", [P, J, D])
        xT = sb("xT", [P, KD, L])
        state = sb("state", [P, KD, L])
        stats = sb("stats", [P, 4, J, 6])
        mean_var = sb("mean_var", [P, 4, J, 2])
        rstd = sb("rstd", [P, 4, J])
        x_op = sb("x_op", [P, KD, L])
        h_even, h_odd = sb("h_even", [P, KH, L]), sb("h_odd", [P, KH, L])
        h_op = [h_even, h_odd, h_even]
        tanh_u = [sb(f"tanh_u{i}", [P, L]) for i in range(2)]
        gate = [sb(f"gate{i}", [P, L]) for i in range(2)]
        h0_full = [sb(f"h0_full{i}", [P, L]) for i in range(2)]
        gelu_full = [sb(f"gelu_full{i}", [P, L]) for i in range(2)]

        ffn = [psum(f"ffn{i}") for i in range(4)]
        attn = [psum(f"attn{i}") for i in range(2)]
        down = [psum(f"down{i}") for i in range(2)]

        small_loaded = sem("small_loaded")
        w_loaded = [sem(f"w_loaded{i}") for i in range(STAGES)]
        w_cast = sem("w_cast")
        w_checked = sem("w_checked")
        w_exact = sem("w_exact")
        pool_step = sem("pool_step")
        consts = sem("consts")
        ident_made = sem("ident_made")
        x_loaded = [sem(f"x_loaded{i}") for i in range(2)]
        x_used = sem("x_used")
        stats_done = [sem(f"stats_done{i}") for i in range(4)]
        var_done = [sem(f"var_done{i}") for i in range(4)]
        var_eps = [sem(f"var_eps{i}") for i in range(4)]
        rstd_done = [sem(f"rstd_done{i}") for i in range(4)]
        ln1_out = sem("ln1_out")
        turn1_done = sem("turn1_done")
        xT_ready = sem("xT_ready")
        drive_done = sem("drive_done")
        state_ready = sem("state_ready")
        readout_done = sem("readout_done")
        y_ready = sem("y_ready")
        y_normed = sem("y_normed")
        x_mid_ready = sem("x_mid_ready")
        ln2_out = sem("ln2_out")
        turn2_done = sem("turn2_done")
        x_hi = sem("x_hi")
        x_split = sem("x_split")
        up_done = sem("up_done")
        tanh_done = sem("tanh_done")
        gate_done = sem("gate_done")
        h0_done = sem("h0_done")
        h0_hi = sem("h0_hi")
        h0_split = sem("h0_split")
        mix_done = sem("mix_done")
        gelu_done = sem("gelu_done")
        g_hi = sem("g_hi")
        mix_split = [sem("h1_split"), sem("h2_split")]
        down_done = sem("down_done")
        z_ready = sem("z_ready")
        z_normed = sem("z_normed")
        out_ready = sem("out_ready")
        stored = [sem(f"stored{i}") for i in range(2)]
        verdict_step = sem("verdict_step")
        verdict = sem("verdict")

        block = ctx.enter_context(nc.Block())

        def hi(op, k):
            return op[:, 0:op.shape[1] // 2, :].rearrange("p k n -> p (k n)").bitcast(F16)[:, k * L:(k + 1) * L]

        def lo(op, k):
            return op[:, op.shape[1] // 2:, :].rearrange("p k n -> p (k n)").bitcast(F16)[:, k * L:(k + 1) * L]

        def tiles(eng, exact, body):
            base = PAIRS * exact
            body(Tile(base, 0), True, False)
            body(Tile(base, 1), False, False)
            with eng.Fori(base + 1, base + PAIRS - 1) as pair:
                body(Tile(pair, 0), False, False)
                body(Tile(pair, 1), False, False)
            body(Tile(base + PAIRS - 1, 0), False, False)
            body(Tile(base + PAIRS - 1, 1), False, True)

        def both_passes(eng, one_pass):
            one_pass(0)
            eng.wait_ge(verdict, 1)
            is_fine = eng.value_load(fine[0:1, 0:1], min_val=0, max_val=1)
            with eng.If(is_fine == 0):
                one_pass(1)

        @block.sync
        def _(sp):
            def load_x(exact, t):
                sp.dma_start(x_in[t.par][:, :, :], x[t.n - NT * exact].rearrange("(j p) d -> p j d", p=P)) \
                    .then_inc(x_loaded[t.par], 16)

            def load_w(n):
                slot = n % STAGES
                at = WCOLS // 2 + slot * WC
                if n >= STAGES:
                    sp.wait_ge(w_checked, n - STAGES + 1)
                sp.dma_start(w_f32[:, at:at + WC], w_all[:, n * WC:(n + 1) * WC]).then_inc(w_loaded[slot], 16)

            def store(exact, t):
                sp.wait_ge(out_ready, t.n + 1)
                sp.dma_start(out[t.n - NT * exact].rearrange("(j p) d -> p j d", p=P), x_out[t.par][:, :, :]) \
                    .then_inc(stored[t.par], 16)

            def one_pass(exact):
                base = PAIRS * exact
                load_x(exact, Tile(base, 0))
                if exact:
                    sp.dma_start(w_f32[:, :], w_all[:, :]).then_inc(w_exact, 16)
                else:
                    sp.dma_start(bw_sb[:, :, :, :], bw).then_inc(small_loaded, 16)
                    sp.dma_start(a_sb[:, :], a_cols).then_inc(small_loaded, 16)
                    sp.dma_start(s_sb[:, :, :], s_cols).then_inc(small_loaded, 16)
                    sp.dma_start(rows_sb[:, :, :].rearrange("p a d -> p (a d)"),
                                 rows.partition_broadcast(P)).then_inc(small_loaded, 16)
                    for n in range(STAGES):
                        load_w(n)
                load_x(exact, Tile(base, 1))
                if not exact:
                    for n in range(STAGES, NWC):
                        load_w(n)

                def body(t, first, last):
                    if not first:
                        store(exact, t.prev())
                    if not last:
                        sp.wait_ge(x_used, t.n + 1)
                        ahead = t.next().next()
                        load_x(exact, ahead)

                body(Tile(base, 0), True, False)
                body(Tile(base, 1), False, False)
                with sp.Fori(base + 1, base + PAIRS - 1) as pair:
                    body(Tile(pair, 0), False, False)
                    body(Tile(pair, 1), False, False)
                end = Tile(base + PAIRS - 1, 0)
                store(exact, end.prev())
                store(exact, end)
                store(exact, end.next())
                for s in stored:
                    sp.wait_ge(s, 16 * (base + PAIRS))

            both_passes(sp, one_pass)

        @block.gpsimd
        def _(pool):
            pool.memset(ident[:, :], 0.0).then_inc(pool_step, 1)
            pool.memset(ones[:, :], 1.0).then_inc(ident_made, 1)
            pool.memset(eps[:, :], EPS).then_inc(pool_step, 1)
            pool.memset(minus_half[:, :], -0.5).then_inc(pool_step, 1)
            pool.memset(agreed[:, :], 0.0).then_inc(pool_step, 1)
            pool.wait_ge(pool_step, 4)
            pool.affine_select(out=ident[:, :], in_=ident[:, :], compare_op=ALU.not_equal, fill=1.0, base=0,
                               pattern=[[-1, P]], channel_multiplier=1).then_inc(ident_made, 1)
            def check_w(n):
                at = WCOLS // 2 + n % STAGES * WC
                pool.wait_ge(w_cast, n + 1)
                pool.wait_ge(w_loaded[n % STAGES], 16 * (n // STAGES + 1))
                staged = w_f32[:, at:at + WC]
                pool.tensor_tensor(staged, staged, w_f16[:, n * WC:(n + 1) * WC], ALU.subtract) \
                    .then_inc(pool_step, 1)
                pool.wait_ge(pool_step, 5 + 3 * n)
                pool.tensor_scalar(agrees[:, :], staged, 0.0, None, ALU.is_equal).then_inc(pool_step, 1)
                pool.wait_ge(pool_step, 6 + 3 * n)
                pool.tensor_tensor(agreed[:, :], agreed[:, :], agrees[:, :], ALU.add).then_inc(pool_step, 1)
                pool.wait_ge(pool_step, 7 + 3 * n)
                pool.sem_inc(w_checked, 1)

            def one_pass(exact):
                def rstd_of(kind, t):
                    pool.wait_ge(var_done[kind], t.n + 1)
                    pool.tensor_tensor(var_plus[:, kind, :], mean_var[:, kind, :, 1], eps[:, :], ALU.add) \
                        .then_inc(var_eps[kind], 1)
                    pool.wait_ge(var_eps[kind], t.n + 1)
                    pool.tensor_tensor(rstd[:, kind, :], var_plus[:, kind, :], minus_half[:, :], ALU.pow) \
                        .then_inc(rstd_done[kind], 1)

                def body(t, first, last):
                    if first and not exact:
                        for n in range(PIECES_H1):
                            check_w(n)
                    if not last:
                        rstd_of(0, t.next())
                    if not first:
                        rstd_of(3, t.prev())
                    if first and not exact:
                        for n in range(PIECES_H1, NWC):
                            check_w(n)
                    if not last:
                        rstd_of(1, t.next())
                        rstd_of(2, t.next())
                    if last:
                        rstd_of(3, t)

                head = Tile(PAIRS * exact, 0)
                rstd_of(0, head)
                rstd_of(1, head)
                rstd_of(2, head)
                tiles(pool, exact, body)

            both_passes(pool, one_pass)

        @block.tensor
        def _(pe):
            def one_pass(exact):
                def product(bank, w_at, op, k, start, stop):
                    if exact:
                        return pe.matmul(bank, w_f32[:, w_at:w_at + P], op[:, k, :], start=start, stop=stop)
                    w = w_f16[:, w_at:w_at + P]
                    pe.matmul(bank, w, hi(op, k), start=start, stop=False)
                    return pe.matmul(bank, w, lo(op, k), start=False, stop=stop)

                def turn(done, ready, count):
                    pe.wait_ge(ready, count)
                    for k in range(KD):
                        for j in range(J):
                            mm = pe.transpose(attn[k][:, j * P:(j + 1) * P], normed[:, j, k * P:(k + 1) * P],
                                              ident[:, :])
                    mm.then_inc(done, 1)

                def turn1(t):
                    turn(turn1_done, ln1_out, t.n + 1)

                def turn2(t):
                    turn(turn2_done, ln2_out, t.n + 1)

                def drive(t):
                    pe.wait_ge(xT_ready, KD * t.n + KD)
                    for c in range(KD):
                        for k in range(KD):
                            mm = pe.matmul(attn[c][:, :], bw_sb[:, 0, k, c * P:(c + 1) * P], xT[:, k, :],
                                           start=(k == 0), stop=(k == KD - 1))
                        mm.then_inc(drive_done, 1)

                def readout(t):
                    pe.wait_ge(state_ready, KD * t.n + KD)
                    for j in range(J):
                        for k in range(KD):
                            mm = pe.matmul(attn[j // 2][:, j % 2 * D:(j % 2 + 1) * D],
                                           state[:, k, j * P:(j + 1) * P], bw_sb[:, 1, k, :],
                                           start=(k == 0), stop=(k == KD - 1))
                    mm.then_inc(readout_done, 1)

                def up(t, c):
                    if c >= 2:
                        pe.wait_ge(h0_done, KH * t.n + c - 1)
                    for half, at in enumerate((W1, W2)):
                        for k in range(KD):
                            if c == 0 and half == 0:
                                pe.wait_ge(x_split, KD * t.n + k + 1)
                            mm = product(ffn[2 * (c % 2) + half][:, :], at + k * HID + c * P, x_op, k,
                                         k == 0, k == KD - 1)
                    mm.then_inc(up_done, 1)

                def mix(t, layer, c):
                    n = layer * KH + c
                    if layer == 0 and c in (0, 2):
                        pe.wait_ge(h0_done, KH * t.n + KH - 1 + c // 2)
                    if n >= 4:
                        pe.wait_ge(gelu_done, 2 * KH * t.n + n - 3)
                    for k in range(KH):
                        if c == 0:
                            pe.wait_ge((h0_split, mix_split[0])[layer], KH * t.n + k + 1)
                        mm = product(ffn[c % 4][:, :], (H1, H2)[layer] + k * HID + c * P, h_op[layer], k,
                                     k == 0, k == KH - 1)
                    mm.then_inc(mix_done, 1)

                def down_part(t, j, fresh):
                    if j == 0 and not fresh:
                        pe.wait_ge(z_ready, t.n)
                    bank = down[j // 2][:, j % 2 * D:(j % 2 + 1) * D]
                    for k in range(KH):
                        if j == 0:
                            pe.wait_ge(mix_split[1], KH * t.n + k + 1)
                        if exact:
                            mm = pe.matmul(bank, h_op[2][:, k, j * P:(j + 1) * P],
                                           w_f32[:, W3 + k * D:W3 + (k + 1) * D], start=(k == 0), stop=(k == KH - 1))
                        else:
                            w = w_f16[:, W3 + k * D:W3 + (k + 1) * D]
                            pe.matmul(bank, hi(h_op[2], k)[:, j * P:(j + 1) * P], w, start=(k == 0), stop=False)
                            mm = pe.matmul(bank, lo(h_op[2], k)[:, j * P:(j + 1) * P], w, start=False,
                                           stop=(k == KH - 1))
                    if j == J - 1:
                        mm.then_inc(down_done, 1)

                def body(t, first, last):
                    fresh = first and not exact
                    if fresh:
                        pe.wait_ge(w_cast, PIECES_UP)
                    for c in range(KH):
                        up(t, c)
                    if fresh:
                        pe.wait_ge(w_cast, PIECES_H1)
                    for c in range(KH):
                        mix(t, 0, c)
                        if not last:
                            if c == 1:
                                turn1(t.next())
                            if c == 2:
                                drive(t.next())
                            if c == 5:
                                readout(t.next())
                    if fresh:
                        pe.wait_ge(w_cast, PIECES_H2)
                    for c in range(KH):
                        mix(t, 1, c)
                        if not last and c == 5:
                            turn2(t.next())
                    if fresh:
                        pe.wait_ge(w_cast, NWC)
                    for j in range(J):
                        down_part(t, j, fresh)

                head = Tile(PAIRS * exact, 0)
                if exact:
                    pe.wait_ge(w_exact, 16)
                else:
                    pe.wait_ge(ident_made, 2)
                    pe.wait_ge(small_loaded, 64)
                turn1(head)
                drive(head)
                readout(head)
                turn2(head)
                tiles(pe, exact, body)
                if not exact:
                    pe.wait_ge(consts, 9)
                    pe.matmul(attn[0][0:1, 0:1], bad_sum[:, :], ones[:, :], start=True, stop=True) \
                        .then_inc(ident_made, 1)

            both_passes(pe, one_pass)

        @block.scalar
        def _(act):
            def one_pass(exact):
                def turn1_copy(t):
                    act.wait_ge(turn1_done, t.n + 1)
                    for k in range(KD):
                        act.activation(xT[:, k, :], attn[k][:, :], ACT.Copy).then_inc(xT_ready, 1)

                def turn2_hi(t):
                    if exact:
                        return
                    act.wait_ge(turn2_done, t.n + 1)
                    for k in range(KD):
                        act.activation(hi(x_op, k), attn[k][:, :], ACT.Copy, scale=2.0 ** A_X).then_inc(x_hi, 1)

                def tanh(t, c):
                    act.wait_ge(up_done, KH * t.n + c + 1)
                    if c >= 2:
                        act.wait_ge(gate_done, KH * t.n + c - 1)
                    act.activation(tanh_u[c % 2][:, :], ffn[2 * (c % 2)][:, :], ACT.Tanh,
                                   scale=tanh_scale[:, c:c + 1]).then_inc(tanh_done, 1)

                def h0_hi_part(t, c):
                    if exact:
                        return
                    act.wait_ge(h0_done, KH * t.n + c + 1)
                    act.activation(hi(h_op[0], c), h0_full[c % 2][:, :], ACT.Copy).then_inc(h0_hi, 1)

                def gelu(t, layer, c):
                    act.wait_ge(mix_done, 2 * KH * t.n + layer * KH + c + 1)
                    if c >= 2:
                        act.wait_ge(mix_split[layer], KH * t.n + c - 1)
                    act.activation(gelu_full[c % 2][:, :], ffn[c % 4][:, :], ACT.Gelu,
                                   scale=mix_scale[:, layer, c:c + 1]).then_inc(gelu_done, 1)

                def body(t, first, last):
                    for c in range(KH):
                        tanh(t, c)
                        if c:
                            h0_hi_part(t, c - 1)
                    h0_hi_part(t, KH - 1)
                    for c in range(KH):
                        gelu(t, 0, c)
                        if not last and c == 1:
                            turn1_copy(t.next())
                    for c in range(KH):
                        gelu(t, 1, c)
                        if not last and c == 5:
                            turn2_hi(t.next())

                head = Tile(PAIRS * exact, 0)
                turn1_copy(head)
                turn2_hi(head)
                if not exact:
                    act.wait_ge(consts, 7)
                tiles(act, exact, body)

            both_passes(act, one_pass)

        @block.vector
        def _(dve):
            def cast_w(n):
                at = WCOLS // 2 + n % STAGES * WC
                dve.wait_ge(w_loaded[n % STAGES], 16 * (n // STAGES + 1))
                dve.tensor_copy(w_f16[:, n * WC:(n + 1) * WC], w_f32[:, at:at + WC]).then_inc(w_cast, 1)

            def statistics(kind, t, src):
                for j in range(J):
                    ins = dve.bn_stats(stats[:, kind, j, :], src[:, j, :])
                ins.then_inc(stats_done[kind], 1)
                dve.wait_ge(stats_done[kind], t.n + 1)
                dve.memset(scratch[:, :], 0.0)
                for j in range(J):
                    ins = dve.bn_aggr(mean_var[:, kind, j, :], stats[:, kind, j, :])
                ins.then_inc(var_done[kind], 1)

            def normalise(kind, t, dst, src):
                dve.wait_ge(rstd_done[kind], t.n + 1)
                for j in range(J):
                    ins = dve.tensor_scalar(dst[:, j, :], src[:, j, :], mean_var[:, kind, j, 0:1],
                                            rstd[:, kind, j:j + 1], ALU.subtract, ALU.mult)
                return ins

            def one_pass(exact):
                def split(op, k, src, power, split_done):
                    if exact:
                        dve.tensor_scalar(op[:, k, :], src, 2.0 ** power, None, ALU.mult).then_inc(split_done, 1)
                    else:
                        dve.scalar_tensor_tensor(out=lo(op, k), in0=src, scalar=2.0 ** power, in1=hi(op, k),
                                                 op0=ALU.mult, op1=ALU.subtract).then_inc(split_done, 1)

                def ln1(t):
                    dve.wait_ge(x_loaded[t.par], 16 * (t.pair + 1))
                    statistics(0, t, x_in[t.par])
                    normalise(0, t, normed, x_in[t.par]).then_inc(ln1_out, 1)

                def scan(t):
                    for c in range(KD):
                        dve.wait_ge(drive_done, KD * t.n + c + 1)
                        dve.tensor_tensor_scan(state[:, c, :], a_wide[:, c, :], attn[c][:, :], 0.0,
                                               ALU.mult, ALU.add).then_inc(state_ready, 1)

                def y_stage(t):
                    dve.wait_ge(readout_done, t.n + 1)
                    for h in range(2):
                        ins = dve.tensor_tensor(y_sb[:, 2 * h:2 * h + 2, :],
                                                attn[h][:, :].rearrange("p (a d) -> p a d", a=2),
                                                b_wide[:, :, :], ALU.add)
                    ins.then_inc(y_ready, 1)
                    dve.wait_ge(y_ready, t.n + 1)
                    statistics(1, t, y_sb)

                def mid_stage(t):
                    normalise(1, t, y_sb, y_sb).then_inc(y_normed, 1)
                    dve.wait_ge(y_normed, t.n + 1)
                    dve.tensor_tensor(x_mid[t.par][:, :, :], x_in[t.par][:, :, :], y_sb[:, :, :], ALU.add) \
                        .then_inc(x_used, 1)
                    dve.wait_ge(x_used, t.n + 1)
                    statistics(2, t, x_mid[t.par])

                def ln2(t):
                    normalise(2, t, normed, x_mid[t.par]).then_inc(ln2_out, 1)

                def x_lo(t):
                    dve.wait_ge(turn2_done, t.n + 1)
                    for k in range(KD):
                        if not exact:
                            dve.wait_ge(x_hi, KD * t.n + k + 1)
                        split(x_op, k, attn[k][:, :], A_X, x_split)

                def h0(t, c):
                    dve.wait_ge(tanh_done, KH * t.n + c + 1)
                    dve.scalar_tensor_tensor(out=gate[c % 2][:, :], in0=tanh_u[c % 2][:, :], scalar=1.0,
                                             in1=ffn[2 * (c % 2)][:, :], op0=ALU.add, op1=ALU.mult) \
                        .then_inc(gate_done, 1)
                    dve.wait_ge(gate_done, KH * t.n + c + 1)
                    dve.scalar_tensor_tensor(out=h0_full[c % 2][:, :], in0=ffn[2 * (c % 2) + 1][:, :],
                                             scalar=gate_scale[:, c:c + 1], in1=gate[c % 2][:, :],
                                             op0=ALU.mult, op1=ALU.mult).then_inc(h0_done, 1)

                def h0_lo(t, c):
                    if exact:
                        dve.wait_ge(h0_done, KH * t.n + c + 1)
                    else:
                        dve.wait_ge(h0_hi, KH * t.n + c + 1)
                    split(h_op[0], c, h0_full[c % 2][:, :], 0, h0_split)

                def gelu_split(t, layer, c):
                    power = (A_H1, A_H2)[layer]
                    n = 2 * KH * t.n + layer * KH + c + 1
                    dve.wait_ge(gelu_done, n)
                    if not exact:
                        dve.tensor_scalar(hi(h_op[1 + layer], c), gelu_full[c % 2][:, :], 2.0 ** power, None,
                                          ALU.mult).then_inc(g_hi, 1)
                        dve.wait_ge(g_hi, n)
                    split(h_op[1 + layer], c, gelu_full[c % 2][:, :], power, mix_split[layer])

                def z_stage(t):
                    dve.wait_ge(down_done, t.n + 1)
                    for h in range(2):
                        ins = dve.tensor_tensor(z_sb[:, 2 * h:2 * h + 2, :],
                                                down[h][:, :].rearrange("p (a d) -> p a d", a=2),
                                                s3_wide[:, :, :], ALU.mult)
                    ins.then_inc(z_ready, 1)
                    dve.wait_ge(z_ready, t.n + 1)
                    statistics(3, t, z_sb)

                def out_stage(t, first_of_parity):
                    if not exact:
                        dve.wait_ge(rstd_done[3], t.n + 1)
                        dve.scalar_tensor_tensor(out=bad[:, 0:J], in0=mean_var[:, 3, :, 1], scalar=0.0,
                                                 in1=bad[:, 0:J], op0=ALU.mult, op1=ALU.add)
                    normalise(3, t, z_sb, z_sb).then_inc(z_normed, 1)
                    dve.wait_ge(z_normed, t.n + 1)
                    if not first_of_parity:
                        dve.wait_ge(stored[t.par], 16 * t.pair)
                    dve.tensor_tensor(x_out[t.par][:, :, :], x_mid[t.par][:, :, :], z_sb[:, :, :], ALU.add) \
                        .then_inc(out_ready, 1)

                def body(t, first, last):
                    for c in range(KH):
                        h0(t, c)
                        if c:
                            h0_lo(t, c - 1)
                    h0_lo(t, KH - 1)
                    if first and not exact:
                        for n in range(PIECES_UP, PIECES_H1):
                            cast_w(n)
                    if not last:
                        ln1(t.next())
                    for c in range(KH):
                        gelu_split(t, 0, c)
                        if c == 0 and not first:
                            z_stage(t.prev())
                        if c == 1 and not first:
                            out_stage(t.prev(), False)
                        if c == 1 and first and not exact:
                            for n in range(PIECES_H1, NWC):
                                cast_w(n)
                        if not last:
                            if c == 3:
                                scan(t.next())
                            if c == 6:
                                y_stage(t.next())
                            if c == 7:
                                mid_stage(t.next())
                    for c in range(KH):
                        gelu_split(t, 1, c)
                        if not last:
                            if c == 1:
                                ln2(t.next())
                            if c == 6:
                                x_lo(t.next())
                    if last:
                        z_stage(t)
                        out_stage(t, False)

                head = Tile(PAIRS * exact, 0)
                ln1(head)
                if not exact:
                    dve.wait_ge(small_loaded, 64)
                    for c in range(KD):
                        dve.tensor_scalar(a_wide[:, c, :], x_in[0][:, 0:2, :].rearrange("p a d -> p (a d)"),
                                          0.0, a_sb[:, c:c + 1], ALU.mult, ALU.add).then_inc(consts, 1)
                    for h in range(2):
                        dve.tensor_copy(b_wide[:, h, :], rows_sb[:, 0, :])
                        dve.tensor_scalar(s3_wide[:, h, :], rows_sb[:, 1, :], 2.0 ** -A_H2, None, ALU.mult)
                    dve.tensor_scalar(tanh_scale[:, :], s_sb[:, 0, :], 2.0 ** -(A_X + 1), None, ALU.mult) \
                        .then_inc(consts, 1)
                    dve.tensor_tensor(ss[:, :], s_sb[:, 0, :], s_sb[:, 1, :], ALU.mult).then_inc(consts, 1)
                    dve.tensor_scalar(mix_scale[:, 0, :], s_sb[:, 2, :], 2.0 ** -A_H0, None, ALU.mult) \
                        .then_inc(consts, 1)
                    dve.tensor_scalar(mix_scale[:, 1, :], s_sb[:, 3, :], 2.0 ** -A_H1, None, ALU.mult) \
                        .then_inc(consts, 1)
                    dve.wait_ge(consts, 6)
                    dve.tensor_scalar(gate_scale[:, :], ss[:, :], 2.0 ** (A_H0 - 2 * A_X - 1), None, ALU.mult) \
                        .then_inc(consts, 1)
                    dve.memset(bad[:, :], 0.0).then_inc(consts, 1)
                    dve.wait_ge(consts, 8)
                scan(head)
                y_stage(head)
                mid_stage(head)
                ln2(head)
                x_lo(head)
                if not exact:
                    for n in range(PIECES_UP):
                        cast_w(n)
                tiles(dve, exact, body)
                if not exact:
                    dve.wait_ge(w_checked, NWC)
                    dve.tensor_reduce(least[:, :], agreed[:, :], AX_X, ALU.min).then_inc(verdict_step, 1)
                    dve.wait_ge(verdict_step, 1)
                    dve.tensor_scalar(bad[:, J:J + 1], least[:, :], -float(NWC), None, ALU.add) \
                        .then_inc(verdict_step, 1)
                    dve.wait_ge(verdict_step, 2)
                    dve.tensor_reduce(bad_sum[:, :], bad[:, :], AX_X, ALU.add).then_inc(consts, 1)
                    dve.wait_ge(ident_made, 3)
                    dve.tensor_scalar(fine[:, :], attn[0][0:1, 0:1], 0.0, None, ALU.is_equal).then_inc(verdict, 1)

            both_passes(dve, one_pass)


def _packed(w):
    import numpy as np
    n_out, n_in = w.shape
    return np.ascontiguousarray(w.T.reshape(n_in // P, P, n_out).transpose(1, 0, 2)).reshape(P, -1)


def kernel(L0_attn_x, L0_attn_A, L0_attn_B, L0_attn_W, L0_attn_b, L0_ffn_w1_w, L0_ffn_w1_s, L0_ffn_w2_w,
           L0_ffn_w2_s, L0_ffn_h1_w, L0_ffn_h1_s, L0_ffn_h2_w, L0_ffn_h2_s, L0_ffn_w3_w, L0_ffn_w3_s):
    import numpy as np
    import concourse.bacc as bacc
    from concourse.bass_utils import run_bass_kernel_spmd

    def columns(v):
        return np.asarray(v).reshape(-1, P).T

    D = L0_attn_x.shape[2]
    arrays = {
        "x_dram": np.ascontiguousarray(L0_attn_x),
        "bw_dram": np.ascontiguousarray(np.stack(
            [_packed(np.asarray(m)).reshape(P, D // P, D) for m in (L0_attn_B, L0_attn_W)], axis=1)),
        "a_dram": np.ascontiguousarray(columns(L0_attn_A)),
        "w_dram": np.ascontiguousarray(np.concatenate(
            [_packed(np.asarray(w)) for w in (L0_ffn_w1_w, L0_ffn_w2_w, L0_ffn_h1_w, L0_ffn_h2_w, L0_ffn_w3_w)],
            axis=1)),
        "s_dram": np.ascontiguousarray(np.stack(
            [columns(s) for s in (L0_ffn_w1_s, L0_ffn_w2_s, L0_ffn_h1_s, L0_ffn_h2_s)], axis=1)),
        "rows_dram": np.ascontiguousarray(np.concatenate([np.asarray(L0_attn_b), np.asarray(L0_ffn_w3_s)])),
    }
    nc = bacc.Bacc("TRN2", target_bir_lowering=False, num_devices=1)
    args = [nc.dram_tensor(name, a.shape, mybir.dt.from_np(a.dtype), kind="ExternalInput").ap()
            for name, a in arrays.items()]
    out = nc.dram_tensor("out_dram", L0_attn_x.shape, F32, kind="ExternalOutput").ap()
    ssm_ffn_kernel(nc, *args, out)
    result = run_bass_kernel_spmd(nc, [arrays], core_ids=[0])
    return result.results[0]["out_dram"]
```

```python
from contextlib import ExitStack

import concourse.bass as bass
from concourse import mybir

P = 128
ALU = mybir.AluOpType
ACT = mybir.ActivationFunctionType
F32 = mybir.dt.float32
F16 = mybir.dt.float16
I32 = mybir.dt.int32
AX_X = mybir.AxisListType.X

EPS = 1e-5
A_X, A_H0, A_H1, A_H2 = 8, 6, 5, 8


class Tile:

    def __init__(self, pair, par):
        self.pair, self.par = pair, par
        self.n = pair * 2 + par

    def next(self):
        return Tile(self.pair, 1) if self.par == 0 else Tile(self.pair + 1, 0)

    def prev(self):
        return Tile(self.pair, 0) if self.par == 1 else Tile(self.pair - 1, 1)


def ssm_ffn_kernel(nc, x, bw, a_cols, w_all, s_cols, rows, out):
    NT, L, D = x.shape
    J = L // P
    KD = D // P
    HID = s_cols.shape[2] * P
    KH = HID // P
    assert KH == 2 * J
    assert NT % 2 == 0 and L == 512 and KD == 2
    PAIRS = NT // 2
    WCOLS = w_all.shape[1]
    W1, W2, H1 = 0, KD * HID, 2 * KD * HID
    H2 = H1 + KH * HID
    W3 = H2 + KH * HID
    assert W3 + KH * D == WCOLS
    WC = 2048
    NWC = WCOLS // WC
    STAGES = (WCOLS // 2) // WC
    SPARE = L * KH // WC
    PIECES_UP = 2 * KD * HID // WC
    PIECES_H1 = PIECES_UP + KH * HID // WC
    PIECES_H2 = PIECES_H1 + KH * HID // WC

    ctx = ExitStack()
    with ctx:
        def sb(name, shape, dt=F32):
            return ctx.enter_context(nc.sbuf_tensor(name, shape, dt))

        def psum(name):
            return ctx.enter_context(nc.psum_tensor(name, [P, 512], F32))

        def sem(name):
            return ctx.enter_context(nc.semaphore(name))

        w_f32 = sb("w_f32", [P, WCOLS])
        w_f16 = w_f32[:, 0:WCOLS // 2].bitcast(F16)
        bw_sb = sb("bw_sb", [P, 2, KD, D])
        a_sb = sb("a_sb", [P, KD])
        a_wide = sb("a_wide", [P, KD, L])
        s_sb = sb("s_sb", [P, 4, KH])
        tanh_scale = sb("tanh_scale", [P, KH])
        gate_scale = sb("gate_scale", [P, KH])
        ss = sb("ss", [P, KH])
        mix_scale = sb("mix_scale", [P, 2, KH])
        rows_sb = sb("rows_sb", [P, 2, D])
        s3_row = sb("s3_row", [P, 1, D])
        ident = sb("ident", [P, P])
        eps = sb("eps", [P, J])
        minus_half = sb("minus_half", [P, J])
        var_plus = sb("var_plus", [P, 4, J])
        ones = sb("ones", [P, 1])
        bad = sb("bad", [P, J + NWC])
        scratch = sb("scratch", [P, 1])
        bad_sum = sb("bad_sum", [P, 1])
        fine = sb("fine", [1, 1], I32)

        x_in = [sb(f"x_in{i}", [P, J, D]) for i in range(2)]
        x_mid = [sb(f"x_mid{i}", [P, J, D]) for i in range(2)]
        x_out = [sb(f"x_out{i}", [P, J, D]) for i in range(2)]
        normed = sb("normed", [P, J, D])
        proj = sb("proj", [P, J, D])
        xT = sb("xT", [P, KD, L])
        state = sb("state", [P, KD, L])
        stats = sb("stats", [P, 4, J, 6])
        mean_var = sb("mean_var", [P, 4, J, 2])
        rstd = sb("rstd", [P, 4, J])
        x_op = sb("x_op", [P, KD, L])
        h_op = [sb(f"h{i}_op", [P, KH, L]) for i in range(3)]
        tanh_u = [sb(f"tanh_u{i}", [P, L]) for i in range(2)]
        gate = [sb(f"gate{i}", [P, L]) for i in range(2)]
        full = [sb(f"full{i}", [P, L]) for i in range(2)]

        ffn = [psum(f"ffn{i}") for i in range(4)]
        attn = [psum(f"attn{i}") for i in range(2)]
        down = [psum(f"down{i}") for i in range(2)]

        small_loaded = sem("small_loaded")
        w_loaded = [sem(f"w_loaded{i}") for i in range(NWC)]
        w_cast = sem("w_cast")
        w_checked = sem("w_checked")
        w_exact = sem("w_exact")
        pool_step = sem("pool_step")
        consts = sem("consts")
        ident_made = sem("ident_made")
        x_loaded = [sem(f"x_loaded{i}") for i in range(2)]
        x_used = sem("x_used")
        stats_done = [sem(f"stats_done{i}") for i in range(4)]
        var_done = [sem(f"var_done{i}") for i in range(4)]
        var_eps = [sem(f"var_eps{i}") for i in range(4)]
        rstd_done = [sem(f"rstd_done{i}") for i in range(4)]
        ln1_out = sem("ln1_out")
        turn1_done = sem("turn1_done")
        xT_ready = sem("xT_ready")
        drive_done = sem("drive_done")
        state_ready = sem("state_ready")
        readout_done = sem("readout_done")
        y_ready = sem("y_ready")
        y_normed = sem("y_normed")
        x_mid_ready = sem("x_mid_ready")
        ln2_out = sem("ln2_out")
        turn2_done = sem("turn2_done")
        x_hi = sem("x_hi")
        x_split = sem("x_split")
        up_done = sem("up_done")
        tanh_done = sem("tanh_done")
        gate_done = sem("gate_done")
        h0_done = sem("h0_done")
        h0_hi = sem("h0_hi")
        h0_split = sem("h0_split")
        mix_done = sem("mix_done")
        gelu_done = sem("gelu_done")
        g_hi = sem("g_hi")
        mix_split = [sem("h1_split"), sem("h2_split")]
        down_done = sem("down_done")
        z_ready = sem("z_ready")
        z_normed = sem("z_normed")
        out_ready = sem("out_ready")
        stored = [sem(f"stored{i}") for i in range(2)]
        verdict = sem("verdict")

        block = ctx.enter_context(nc.Block())

        def hi(op, k):
            return op[:, 0:op.shape[1] // 2, :].rearrange("p k n -> p (k n)").bitcast(F16)[:, k * L:(k + 1) * L]

        def lo(op, k):
            return op[:, op.shape[1] // 2:, :].rearrange("p k n -> p (k n)").bitcast(F16)[:, k * L:(k + 1) * L]

        def staged(n):
            if STAGES <= n < STAGES + SPARE:
                return h_op[2][:, :, :].rearrange("p k n -> p (k n)")[:, (n - STAGES) * WC:(n - STAGES + 1) * WC]
            at = WCOLS // 2 + (n if n < STAGES else n - STAGES - SPARE) * WC
            return w_f32[:, at:at + WC]

        def tiles(eng, exact, body):
            base = PAIRS * exact
            body(Tile(base, 0), True, False)
            body(Tile(base, 1), False, False)
            with eng.Fori(base + 1, base + PAIRS - 1) as pair:
                body(Tile(pair, 0), False, False)
                body(Tile(pair, 1), False, False)
            body(Tile(base + PAIRS - 1, 0), False, False)
            body(Tile(base + PAIRS - 1, 1), False, True)

        def both_passes(eng, one_pass):
            one_pass(0)
            eng.wait_ge(verdict, 1)
            is_fine = eng.value_load(fine[0:1, 0:1], min_val=0, max_val=1)
            with eng.If(is_fine == 0):
                one_pass(1)

        @block.sync
        def _(sp):
            def load_x(exact, t):
                sp.dma_start(x_in[t.par][:, :, :], x[t.n - NT * exact].rearrange("(j p) d -> p j d", p=P)) \
                    .then_inc(x_loaded[t.par], 16)

            def load_w(n):
                if n >= STAGES + SPARE:
                    sp.wait_ge(w_checked, n - STAGES - SPARE + 1)
                sp.dma_start(staged(n), w_all[:, n * WC:(n + 1) * WC]).then_inc(w_loaded[n], 16)

            def store(exact, t):
                sp.wait_ge(out_ready, t.n + 1)
                sp.dma_start(out[t.n - NT * exact].rearrange("(j p) d -> p j d", p=P), x_out[t.par][:, :, :]) \
                    .then_inc(stored[t.par], 16)

            def one_pass(exact):
                base = PAIRS * exact
                load_x(exact, Tile(base, 0))
                if exact:
                    sp.dma_start(w_f32[:, :], w_all[:, :]).then_inc(w_exact, 16)
                else:
                    sp.dma_start(bw_sb[:, :, :, :], bw).then_inc(small_loaded, 16)
                    sp.dma_start(a_sb[:, :], a_cols).then_inc(small_loaded, 16)
                    sp.dma_start(s_sb[:, :, :], s_cols).then_inc(small_loaded, 16)
                    sp.dma_start(rows_sb[:, :, :].rearrange("p a d -> p (a d)"),
                                 rows.partition_broadcast(P)).then_inc(small_loaded, 16)
                    for n in range(PIECES_H1):
                        load_w(n)
                load_x(exact, Tile(base, 1))
                if not exact:
                    for n in range(PIECES_H1, NWC):
                        load_w(n)

                def body(t, first, last):
                    if not first:
                        store(exact, t.prev())
                    if not last:
                        sp.wait_ge(x_used, t.n + 1)
                        ahead = t.next().next()
                        load_x(exact, ahead)

                body(Tile(base, 0), True, False)
                body(Tile(base, 1), False, False)
                with sp.Fori(base + 1, base + PAIRS - 1) as pair:
                    body(Tile(pair, 0), False, False)
                    body(Tile(pair, 1), False, False)
                end = Tile(base + PAIRS - 1, 0)
                store(exact, end.prev())
                store(exact, end)
                store(exact, end.next())
                for s in stored:
                    sp.wait_ge(s, 16 * (base + PAIRS))

            both_passes(sp, one_pass)

        @block.gpsimd
        def _(pool):
            pool.memset(ident[:, :], 0.0).then_inc(pool_step, 1)
            pool.memset(ones[:, :], 1.0).then_inc(ident_made, 1)
            pool.memset(eps[:, :], EPS).then_inc(pool_step, 1)
            pool.memset(minus_half[:, :], -0.5).then_inc(pool_step, 1)
            pool.wait_ge(pool_step, 3)
            pool.affine_select(out=ident[:, :], in_=ident[:, :], compare_op=ALU.not_equal, fill=1.0, base=0,
                               pattern=[[-1, P]], channel_multiplier=1).then_inc(ident_made, 1)
            def one_pass(exact):
                def rstd_of(kind, t):
                    pool.wait_ge(var_done[kind], t.n + 1)
                    pool.tensor_tensor(var_plus[:, kind, :], mean_var[:, kind, :, 1], eps[:, :], ALU.add) \
                        .then_inc(var_eps[kind], 1)
                    pool.wait_ge(var_eps[kind], t.n + 1)
                    pool.tensor_tensor(rstd[:, kind, :], var_plus[:, kind, :], minus_half[:, :], ALU.pow) \
                        .then_inc(rstd_done[kind], 1)

                def body(t, first, last):
                    if not first:
                        rstd_of(3, t.prev())
                    if not last:
                        rstd_of(0, t.next())
                    if not last:
                        rstd_of(1, t.next())
                        rstd_of(2, t.next())
                    if last:
                        rstd_of(3, t)

                head = Tile(PAIRS * exact, 0)
                rstd_of(0, head)
                rstd_of(1, head)
                rstd_of(2, head)
                tiles(pool, exact, body)

            both_passes(pool, one_pass)

        @block.tensor
        def _(pe):
            def one_pass(exact):
                def product(bank, w_at, op, k, start, stop):
                    if exact:
                        return pe.matmul(bank, w_f32[:, w_at:w_at + P], op[:, k, :], start=start, stop=stop)
                    w = w_f16[:, w_at:w_at + P]
                    pe.matmul(bank, w, hi(op, k), start=start, stop=False)
                    return pe.matmul(bank, w, lo(op, k), start=False, stop=stop)

                def turn(done, ready, count):
                    pe.wait_ge(ready, count)
                    for k in range(KD):
                        for j in range(J):
                            mm = pe.transpose(attn[k][:, j * P:(j + 1) * P], normed[:, j, k * P:(k + 1) * P],
                                              ident[:, :])
                    mm.then_inc(done, 1)

                def turn1(t):
                    turn(turn1_done, ln1_out, t.n + 1)

                def turn2(t):
                    turn(turn2_done, ln2_out, t.n + 1)

                def drive(t):
                    pe.wait_ge(xT_ready, KD * t.n + KD)
                    for c in range(KD):
                        for k in range(KD):
                            mm = pe.matmul(attn[c][:, :], bw_sb[:, 0, k, c * P:(c + 1) * P], xT[:, k, :],
                                           start=(k == 0), stop=(k == KD - 1))
                        mm.then_inc(drive_done, 1)

                def readout(t):
                    pe.wait_ge(state_ready, KD * t.n + KD)
                    for j in range(J):
                        for k in range(KD):
                            mm = pe.matmul(attn[j // 2][:, j % 2 * D:(j % 2 + 1) * D],
                                           state[:, k, j * P:(j + 1) * P], bw_sb[:, 1, k, :],
                                           start=(k == 0), stop=(k == KD - 1))
                    mm.then_inc(readout_done, 1)

                def up(t, c, head=False):
                    if c >= 2:
                        pe.wait_ge(h0_done, KH * t.n + c - 1)
                    elif not head:
                        pe.wait_ge(gelu_done, 2 * KH * t.n - 2 + 2 * c)
                    for half, at in enumerate((W1, W2)):
                        for k in range(KD):
                            if c == 0 and half == 0:
                                pe.wait_ge(x_split, KD * t.n + k + 1)
                            mm = product(ffn[2 * (c % 2) + half][:, :], at + k * HID + c * P, x_op, k,
                                         k == 0, k == KD - 1)
                    mm.then_inc(up_done, 1)

                def mix(t, layer, c):
                    n = layer * KH + c
                    if layer == 0 and c in (0, 2):
                        pe.wait_ge(h0_done, KH * t.n + KH - 1 + c // 2)
                    if n >= 4:
                        pe.wait_ge(gelu_done, 2 * KH * t.n + n - 3)
                    for k in range(KH):
                        if c == 0:
                            pe.wait_ge((h0_split, mix_split[0])[layer], KH * t.n + k + 1)
                        mm = product(ffn[c % 4][:, :], (H1, H2)[layer] + k * HID + c * P, h_op[layer], k,
                                     k == 0, k == KH - 1)
                    mm.then_inc(mix_done, 1)

                def down_part(t, j, fresh):
                    if j == 0 and not fresh:
                        pe.wait_ge(z_ready, t.n)
                    bank = down[j // 2][:, j % 2 * D:(j % 2 + 1) * D]
                    for k in range(KH):
                        if j == 0:
                            pe.wait_ge(mix_split[1], KH * t.n + k + 1)
                        if exact:
                            mm = pe.matmul(bank, h_op[2][:, k, j * P:(j + 1) * P],
                                           w_f32[:, W3 + k * D:W3 + (k + 1) * D], start=(k == 0), stop=(k == KH - 1))
                        else:
                            w = w_f16[:, W3 + k * D:W3 + (k + 1) * D]
                            pe.matmul(bank, hi(h_op[2], k)[:, j * P:(j + 1) * P], w, start=(k == 0), stop=False)
                            mm = pe.matmul(bank, lo(h_op[2], k)[:, j * P:(j + 1) * P], w, start=False,
                                           stop=(k == KH - 1))
                    if j == J - 1:
                        mm.then_inc(down_done, 1)

                def body(t, first, last):
                    fresh = first and not exact
                    if fresh:
                        pe.wait_ge(w_cast, PIECES_H1)
                    for c in range(KH):
                        mix(t, 0, c)
                        if not last:
                            if c == 4:
                                turn1(t.next())
                            if c == 5:
                                drive(t.next())
                            if c == 6:
                                readout(t.next())
                    if fresh:
                        pe.wait_ge(w_cast, PIECES_H2)
                    for c in range(KH):
                        mix(t, 1, c)
                        if not last and c == 3:
                            turn2(t.next())
                    if fresh:
                        pe.wait_ge(w_cast, NWC)
                    for j in range(J):
                        if not last:
                            up(t.next(), 2 * j)
                            up(t.next(), 2 * j + 1)
                        down_part(t, j, fresh)

                head = Tile(PAIRS * exact, 0)
                if exact:
                    pe.wait_ge(w_exact, 16)
                else:
                    pe.wait_ge(ident_made, 2)
                    pe.wait_ge(small_loaded, 64)
                turn1(head)
                drive(head)
                readout(head)
                turn2(head)
                if not exact:
                    pe.wait_ge(w_cast, PIECES_UP)
                for c in range(KH):
                    up(head, c, head=True)
                tiles(pe, exact, body)
                if not exact:
                    pe.wait_ge(consts, 9)
                    pe.matmul(attn[0][0:1, 0:1], bad_sum[:, :], ones[:, :], start=True, stop=True) \
                        .then_inc(ident_made, 1)

            both_passes(pe, one_pass)

        @block.scalar
        def _(act):
            def cast_w(n):
                act.wait_ge(w_loaded[n], 16)
                act.activation(w_f16[:, n * WC:(n + 1) * WC], staged(n), ACT.Copy).then_inc(w_cast, 1)

            def one_pass(exact):
                def turn1_copy(t):
                    act.wait_ge(turn1_done, t.n + 1)
                    for k in range(KD):
                        act.activation(xT[:, k, :], attn[k][:, :], ACT.Copy).then_inc(xT_ready, 1)

                def turn2_hi(t):
                    if exact:
                        return
                    act.wait_ge(turn2_done, t.n + 1)
                    for k in range(KD):
                        act.activation(hi(x_op, k), attn[k][:, :], ACT.Copy, scale=2.0 ** A_X).then_inc(x_hi, 1)

                def tanh(t, c):
                    act.wait_ge(up_done, KH * t.n + c + 1)
                    if c >= 2:
                        act.wait_ge(gate_done, KH * t.n + c - 1)
                    act.activation(tanh_u[c % 2][:, :], ffn[2 * (c % 2)][:, :], ACT.Tanh,
                                   scale=tanh_scale[:, c:c + 1]).then_inc(tanh_done, 1)

                def h0_hi_part(t, c):
                    if exact:
                        return
                    act.wait_ge(h0_done, KH * t.n + c + 1)
                    act.activation(hi(h_op[0], c), full[c % 2][:, :], ACT.Copy).then_inc(h0_hi, 1)

                def gelu(t, layer, c):
                    act.wait_ge(mix_done, 2 * KH * t.n + layer * KH + c + 1)
                    if c >= 2:
                        act.wait_ge(mix_split[layer], KH * t.n + c - 1)
                    act.activation(full[c % 2][:, :], ffn[c % 4][:, :], ACT.Gelu,
                                   scale=mix_scale[:, layer, c:c + 1]).then_inc(gelu_done, 1)

                def up(t, casts=()):
                    for c in range(KH):
                        tanh(t, c)
                        if c:
                            h0_hi_part(t, c - 1)
                        for n in [n for at, n in casts if at == c]:
                            cast_w(n)
                    h0_hi_part(t, KH - 1)

                def body(t, first, last):
                    for c in range(KH):
                        gelu(t, 0, c)
                        if first and not exact and PIECES_H1 + c < NWC:
                            cast_w(PIECES_H1 + c)
                        if not last and c == 4:
                            turn1_copy(t.next())
                    for c in range(KH):
                        gelu(t, 1, c)
                        if not last and c == 3:
                            turn2_hi(t.next())
                    if not last:
                        up(t.next())

                head = Tile(PAIRS * exact, 0)
                turn1_copy(head)
                if not exact:
                    for n in range(PIECES_UP + 2):
                        cast_w(n)
                turn2_hi(head)
                if not exact:
                    act.wait_ge(consts, 7)
                up(head, () if exact else ((KH // 2, PIECES_UP + 2), (KH - 1, PIECES_UP + 3)))
                tiles(act, exact, body)

            both_passes(act, one_pass)

        @block.vector
        def _(dve):
            def check_w(n):
                dve.wait_ge(w_cast, n + 1)
                dve.scalar_tensor_tensor(out=staged(n), in0=staged(n), scalar=0.0,
                                         in1=w_f16[:, n * WC:(n + 1) * WC], op0=ALU.add, op1=ALU.not_equal,
                                         accum_out=bad[:, J + n:J + n + 1]).then_inc(w_checked, 1)

            def statistics(kind, t, src):
                for j in range(J):
                    ins = dve.bn_stats(stats[:, kind, j, :], src[:, j, :])
                ins.then_inc(stats_done[kind], 1)
                dve.wait_ge(stats_done[kind], t.n + 1)
                dve.memset(scratch[:, :], 0.0)
                for j in range(J):
                    ins = dve.bn_aggr(mean_var[:, kind, j, :], stats[:, kind, j, :])
                ins.then_inc(var_done[kind], 1)

            def normalise(kind, t, dst, src):
                dve.wait_ge(rstd_done[kind], t.n + 1)
                for j in range(J):
                    ins = dve.tensor_scalar(dst[:, j, :], src[:, j, :], mean_var[:, kind, j, 0:1],
                                            rstd[:, kind, j:j + 1], ALU.subtract, ALU.mult)
                return ins

            def one_pass(exact):
                def split(op, k, src, power, split_done):
                    if exact:
                        dve.tensor_scalar(op[:, k, :], src, 2.0 ** power, None, ALU.mult).then_inc(split_done, 1)
                    else:
                        dve.scalar_tensor_tensor(out=lo(op, k), in0=src, scalar=2.0 ** power, in1=hi(op, k),
                                                 op0=ALU.mult, op1=ALU.subtract).then_inc(split_done, 1)

                def ln1_stats(t):
                    dve.wait_ge(x_loaded[t.par], 16 * (t.pair + 1))
                    statistics(0, t, x_in[t.par])

                def ln1(t):
                    normalise(0, t, normed, x_in[t.par]).then_inc(ln1_out, 1)

                def scan(t):
                    for c in range(KD):
                        dve.wait_ge(drive_done, KD * t.n + c + 1)
                        dve.tensor_tensor_scan(state[:, c, :], a_wide[:, c, :], attn[c][:, :], 0.0,
                                               ALU.mult, ALU.add).then_inc(state_ready, 1)

                def y_stage(t):
                    dve.wait_ge(readout_done, t.n + 1)
                    for h in range(2):
                        ins = dve.tensor_tensor(proj[:, 2 * h:2 * h + 2, :],
                                                attn[h][:, :].rearrange("p (a d) -> p a d", a=2),
                                                rows_sb[:, 0:1, :].to_broadcast([P, 2, D]), ALU.add)
                    ins.then_inc(y_ready, 1)
                    dve.wait_ge(y_ready, t.n + 1)
                    statistics(1, t, proj)

                def mid_stage(t):
                    normalise(1, t, proj, proj).then_inc(y_normed, 1)
                    dve.wait_ge(y_normed, t.n + 1)
                    dve.tensor_tensor(x_mid[t.par][:, :, :], x_in[t.par][:, :, :], proj[:, :, :], ALU.add) \
                        .then_inc(x_used, 1)
                    dve.wait_ge(x_used, t.n + 1)
                    statistics(2, t, x_mid[t.par])

                def ln2(t):
                    normalise(2, t, normed, x_mid[t.par]).then_inc(ln2_out, 1)

                def x_lo(t):
                    dve.wait_ge(turn2_done, t.n + 1)
                    for k in range(KD):
                        if not exact:
                            dve.wait_ge(x_hi, KD * t.n + k + 1)
                        split(x_op, k, attn[k][:, :], A_X, x_split)

                def h0(t, c):
                    dve.wait_ge(tanh_done, KH * t.n + c + 1)
                    dve.scalar_tensor_tensor(out=gate[c % 2][:, :], in0=tanh_u[c % 2][:, :], scalar=1.0,
                                             in1=ffn[2 * (c % 2)][:, :], op0=ALU.add, op1=ALU.mult) \
                        .then_inc(gate_done, 1)
                    dve.wait_ge(gate_done, KH * t.n + c + 1)
                    dve.scalar_tensor_tensor(out=full[c % 2][:, :], in0=ffn[2 * (c % 2) + 1][:, :],
                                             scalar=gate_scale[:, c:c + 1], in1=gate[c % 2][:, :],
                                             op0=ALU.mult, op1=ALU.mult).then_inc(h0_done, 1)

                def h0_lo(t, c):
                    if exact:
                        dve.wait_ge(h0_done, KH * t.n + c + 1)
                    else:
                        dve.wait_ge(h0_hi, KH * t.n + c + 1)
                    split(h_op[0], c, full[c % 2][:, :], 0, h0_split)

                def gelu_split(t, layer, c):
                    power = (A_H1, A_H2)[layer]
                    n = 2 * KH * t.n + layer * KH + c + 1
                    dve.wait_ge(gelu_done, n)
                    if not exact:
                        dve.tensor_scalar(hi(h_op[1 + layer], c), full[c % 2][:, :], 2.0 ** power, None,
                                          ALU.mult).then_inc(g_hi, 1)
                        dve.wait_ge(g_hi, n)
                    split(h_op[1 + layer], c, full[c % 2][:, :], power, mix_split[layer])

                def z_stage(t):
                    dve.wait_ge(down_done, t.n + 1)
                    for h in range(2):
                        ins = dve.tensor_tensor(proj[:, 2 * h:2 * h + 2, :],
                                                down[h][:, :].rearrange("p (a d) -> p a d", a=2),
                                                s3_row[:, :, :].to_broadcast([P, 2, D]), ALU.mult)
                    ins.then_inc(z_ready, 1)
                    dve.wait_ge(z_ready, t.n + 1)
                    statistics(3, t, proj)

                def out_stage(t):
                    if not exact:
                        dve.wait_ge(rstd_done[3], t.n + 1)
                        dve.scalar_tensor_tensor(out=bad[:, 0:J], in0=mean_var[:, 3, :, 1], scalar=0.0,
                                                 in1=bad[:, 0:J], op0=ALU.mult, op1=ALU.add)
                    normalise(3, t, proj, proj).then_inc(z_normed, 1)
                    dve.wait_ge(z_normed, t.n + 1)
                    if not (isinstance(t.pair, int) and t.pair == 0):
                        dve.wait_ge(stored[t.par], 16 * t.pair)
                    dve.tensor_tensor(x_out[t.par][:, :, :], x_mid[t.par][:, :, :], proj[:, :, :], ALU.add) \
                        .then_inc(out_ready, 1)

                def up(t):
                    for c in range(KH):
                        h0(t, c)
                        if c:
                            h0_lo(t, c - 1)
                    h0_lo(t, KH - 1)

                def body(t, first, last):
                    checks = {0: (0, 1), 1: (2, 3), 2: (4, 5), 3: (6,)} if first and not exact else {}
                    for c in range(KH):
                        for n in checks.get(c, ()):
                            check_w(n)
                        gelu_split(t, 0, c)
                        if c == 0 and not first:
                            z_stage(t.prev())
                        if c == 1 and not first:
                            out_stage(t.prev())
                        if not last:
                            if c == 2:
                                ln1_stats(t.next())
                            if c == 3:
                                ln1(t.next())
                            if c == 5:
                                scan(t.next())
                            if c == 7:
                                y_stage(t.next())
                    for c in range(KH):
                        gelu_split(t, 1, c)
                        if first and not exact and c >= KH - (NWC - STAGES - SPARE):
                            check_w(NWC - KH + c)
                        if not last:
                            if c == 0:
                                mid_stage(t.next())
                            if c == 1:
                                ln2(t.next())
                            if c == 3:
                                x_lo(t.next())
                    if not last:
                        up(t.next())
                    else:
                        z_stage(t)
                        out_stage(t)

                head = Tile(PAIRS * exact, 0)
                ln1_stats(head)
                ln1(head)
                if not exact:
                    dve.wait_ge(small_loaded, 64)
                    for c in range(KD):
                        dve.tensor_scalar(a_wide[:, c, :], x_in[0][:, 0:2, :].rearrange("p a d -> p (a d)"),
                                          0.0, a_sb[:, c:c + 1], ALU.mult, ALU.add).then_inc(consts, 1)
                    dve.tensor_scalar(s3_row[:, 0, :], rows_sb[:, 1, :], 2.0 ** -A_H2, None, ALU.mult)
                    dve.tensor_scalar(tanh_scale[:, :], s_sb[:, 0, :], 2.0 ** -(A_X + 1), None, ALU.mult) \
                        .then_inc(consts, 1)
                    dve.tensor_tensor(ss[:, :], s_sb[:, 0, :], s_sb[:, 1, :], ALU.mult).then_inc(consts, 1)
                    dve.tensor_scalar(mix_scale[:, 0, :], s_sb[:, 2, :], 2.0 ** -A_H0, None, ALU.mult) \
                        .then_inc(consts, 1)
                    dve.tensor_scalar(mix_scale[:, 1, :], s_sb[:, 3, :], 2.0 ** -A_H1, None, ALU.mult) \
                        .then_inc(consts, 1)
                    dve.wait_ge(consts, 6)
                    dve.tensor_scalar(gate_scale[:, :], ss[:, :], 2.0 ** (A_H0 - 2 * A_X - 1), None, ALU.mult) \
                        .then_inc(consts, 1)
                    dve.memset(bad[:, :], 0.0).then_inc(consts, 1)
                    dve.wait_ge(consts, 8)
                scan(head)
                y_stage(head)
                mid_stage(head)
                ln2(head)
                x_lo(head)
                up(head)
                tiles(dve, exact, body)
                if not exact:
                    dve.wait_ge(out_ready, NT)
                    dve.wait_ge(w_checked, NWC)
                    dve.tensor_reduce(bad_sum[:, :], bad[:, :], AX_X, ALU.add).then_inc(consts, 1)
                    dve.wait_ge(ident_made, 3)
                    dve.tensor_scalar(fine[:, :], attn[0][0:1, 0:1], 0.0, None, ALU.is_equal).then_inc(verdict, 1)

            both_passes(dve, one_pass)


def _packed(w):
    import numpy as np
    n_out, n_in = w.shape
    return np.ascontiguousarray(w.T.reshape(n_in // P, P, n_out).transpose(1, 0, 2)).reshape(P, -1)


def kernel(L0_attn_x, L0_attn_A, L0_attn_B, L0_attn_W, L0_attn_b, L0_ffn_w1_w, L0_ffn_w1_s, L0_ffn_w2_w,
           L0_ffn_w2_s, L0_ffn_h1_w, L0_ffn_h1_s, L0_ffn_h2_w, L0_ffn_h2_s, L0_ffn_w3_w, L0_ffn_w3_s):
    import numpy as np
    import concourse.bacc as bacc
    from concourse.bass_utils import run_bass_kernel_spmd

    def columns(v):
        return np.asarray(v).reshape(-1, P).T

    D = L0_attn_x.shape[2]
    arrays = {
        "x_dram": np.ascontiguousarray(L0_attn_x),
        "bw_dram": np.ascontiguousarray(np.stack(
            [_packed(np.asarray(m)).reshape(P, D // P, D) for m in (L0_attn_B, L0_attn_W)], axis=1)),
        "a_dram": np.ascontiguousarray(columns(L0_attn_A)),
        "w_dram": np.ascontiguousarray(np.concatenate(
            [_packed(np.asarray(w)) for w in (L0_ffn_w1_w, L0_ffn_w2_w, L0_ffn_h1_w, L0_ffn_h2_w, L0_ffn_w3_w)],
            axis=1)),
        "s_dram": np.ascontiguousarray(np.stack(
            [columns(s) for s in (L0_ffn_w1_s, L0_ffn_w2_s, L0_ffn_h1_s, L0_ffn_h2_s)], axis=1)),
        "rows_dram": np.ascontiguousarray(np.concatenate([np.asarray(L0_attn_b), np.asarray(L0_ffn_w3_s)])),
    }
    nc = bacc.Bacc("TRN2", target_bir_lowering=False, num_devices=1)
    args = [nc.dram_tensor(name, a.shape, mybir.dt.from_np(a.dtype), kind="ExternalInput").ap()
            for name, a in arrays.items()]
    out = nc.dram_tensor("out_dram", L0_attn_x.shape, F32, kind="ExternalOutput").ap()
    ssm_ffn_kernel(nc, *args, out)
    result = run_bass_kernel_spmd(nc, [arrays], core_ids=[0])
    return result.results[0]["out_dram"]
```

```python
from contextlib import ExitStack

import concourse.bass as bass
from concourse import mybir

P = 128
ALU = mybir.AluOpType
ACT = mybir.ActivationFunctionType
F32 = mybir.dt.float32
F16 = mybir.dt.float16
I32 = mybir.dt.int32
AX_X = mybir.AxisListType.X

EPS = 1e-5
A_X, A_H0, A_H1, A_H2 = 8, 6, 5, 8


class Tile:

    def __init__(self, pair, par):
        self.pair, self.par = pair, par
        self.n = pair * 2 + par

    def next(self):
        return Tile(self.pair, 1) if self.par == 0 else Tile(self.pair + 1, 0)

    def prev(self):
        return Tile(self.pair, 0) if self.par == 1 else Tile(self.pair - 1, 1)


def ssm_ffn_kernel(nc, x, bw, a_cols, w_all, s_cols, rows, out):
    NT, L, D = x.shape
    J = L // P
    KD = D // P
    HID = s_cols.shape[2] * P
    KH = HID // P
    assert KH == 2 * J
    assert NT % 2 == 0 and L == 512 and KD == 2
    PAIRS = NT // 2
    WCOLS = w_all.shape[1]
    W1, W2, H1 = 0, KD * HID, 2 * KD * HID
    H2 = H1 + KH * HID
    W3 = H2 + KH * HID
    assert W3 + KH * D == WCOLS
    WC = 2048
    NWC = WCOLS // WC
    STAGES = (WCOLS // 2) // WC
    SPARE = L * KH // WC
    PIECES_UP = 2 * KD * HID // WC
    PIECES_H1 = PIECES_UP + KH * HID // WC
    PIECES_H2 = PIECES_H1 + KH * HID // WC

    ctx = ExitStack()
    with ctx:
        def sb(name, shape, dt=F32):
            return ctx.enter_context(nc.sbuf_tensor(name, shape, dt))

        def psum(name):
            return ctx.enter_context(nc.psum_tensor(name, [P, 512], F32))

        def sem(name):
            return ctx.enter_context(nc.semaphore(name))

        w_f32 = sb("w_f32", [P, WCOLS])
        w_f16 = w_f32[:, 0:WCOLS // 2].bitcast(F16)
        bw_sb = sb("bw_sb", [P, 2, KD, D])
        a_sb = sb("a_sb", [P, KD])
        a_wide = sb("a_wide", [P, KD, L])
        s_sb = sb("s_sb", [P, 4, KH])
        tanh_scale = sb("tanh_scale", [P, KH])
        gate_scale = sb("gate_scale", [P, KH])
        ss = sb("ss", [P, KH])
        mix_scale = sb("mix_scale", [P, 2, KH])
        rows_sb = sb("rows_sb", [P, 2, D])
        s3_row = sb("s3_row", [P, 1, D])
        ident = sb("ident", [P, P])
        eps = sb("eps", [P, J])
        minus_half = sb("minus_half", [P, J])
        var_plus = sb("var_plus", [P, 4, J])
        ones = sb("ones", [P, 1])
        bad = sb("bad", [P, NWC + 3 * KH])
        lo_sum = sb("lo_sum", [P, 3 * KH])
        scratch = sb("scratch", [P, 1])
        bad_sum = sb("bad_sum", [P, 1])
        fine = sb("fine", [1, 1], I32)

        x_in = [sb(f"x_in{i}", [P, J, D]) for i in range(2)]
        x_mid = [sb(f"x_mid{i}", [P, J, D]) for i in range(2)]
        x_out = [sb(f"x_out{i}", [P, J, D]) for i in range(2)]
        normed = sb("normed", [P, J, D])
        proj = sb("proj", [P, J, D])
        xT = sb("xT", [P, KD, L])
        state = sb("state", [P, KD, L])
        stats = sb("stats", [P, 4, J, 6])
        mean_var = sb("mean_var", [P, 4, J, 2])
        rstd = sb("rstd", [P, 4, J])
        x_op = sb("x_op", [P, KD, L])
        h_op = [sb(f"h{i}_op", [P, KH, L]) for i in range(3)]
        tanh_u = [sb(f"tanh_u{i}", [P, L]) for i in range(2)]
        gate = [sb(f"gate{i}", [P, L]) for i in range(2)]
        full = [sb(f"full{i}", [P, L]) for i in range(2)]

        ffn = [psum(f"ffn{i}") for i in range(4)]
        attn = [psum(f"attn{i}") for i in range(2)]
        down = [psum(f"down{i}") for i in range(2)]

        bw_loaded = sem("bw_loaded")
        small_loaded = sem("small_loaded")
        w_loaded = [sem(f"w_loaded{i}") for i in range(NWC)]
        w_cast = sem("w_cast")
        w_checked = sem("w_checked")
        w_exact = sem("w_exact")
        pool_step = sem("pool_step")
        zeroed = sem("zeroed")
        consts = sem("consts")
        ident_made = sem("ident_made")
        x_loaded = [[sem(f"x_loaded{i}_{h}") for h in range(2)] for i in range(2)]
        x_used = sem("x_used")
        stats_done = [sem(f"stats_done{i}") for i in range(4)]
        var_done = [sem(f"var_done{i}") for i in range(4)]
        var_eps = [sem(f"var_eps{i}") for i in range(4)]
        rstd_done = [sem(f"rstd_done{i}") for i in range(4)]
        ln1_out = sem("ln1_out")
        turn1_done = sem("turn1_done")
        xT_ready = sem("xT_ready")
        drive_done = sem("drive_done")
        state_ready = sem("state_ready")
        readout_done = sem("readout_done")
        y_ready = sem("y_ready")
        y_normed = sem("y_normed")
        ln2_out = sem("ln2_out")
        turn2_done = sem("turn2_done")
        x_hi = sem("x_hi")
        x_split = sem("x_split")
        up_done = sem("up_done")
        tanh_done = sem("tanh_done")
        gate_done = sem("gate_done")
        h0_done = sem("h0_done")
        h0_hi = sem("h0_hi")
        h0_split = sem("h0_split")
        mix_done = sem("mix_done")
        gelu_done = sem("gelu_done")
        g_hi = sem("g_hi")
        mix_split = [sem("h1_split"), sem("h2_split")]
        down_done = sem("down_done")
        z_ready = sem("z_ready")
        z_normed = sem("z_normed")
        out_ready = sem("out_ready")
        stored = [sem(f"stored{i}") for i in range(2)]
        range_checked = sem("range_checked")
        bad_summed = sem("bad_summed")
        bad_total = sem("bad_total")
        verdict = sem("verdict")

        block = ctx.enter_context(nc.Block())

        def hi(op, k):
            return op[:, 0:op.shape[1] // 2, :].rearrange("p k n -> p (k n)").bitcast(F16)[:, k * L:(k + 1) * L]

        def lo(op, k):
            return op[:, op.shape[1] // 2:, :].rearrange("p k n -> p (k n)").bitcast(F16)[:, k * L:(k + 1) * L]

        def staged(n):
            if STAGES <= n < STAGES + SPARE:
                return h_op[2][:, :, :].rearrange("p k n -> p (k n)")[:, (n - STAGES) * WC:(n - STAGES + 1) * WC]
            at = WCOLS // 2 + (n if n < STAGES else n - STAGES - SPARE) * WC
            return w_f32[:, at:at + WC]

        def tiles(eng, exact, body):
            base = PAIRS * exact
            body(Tile(base, 0), True, 2)
            body(Tile(base, 1), False, 2)
            with eng.Fori(base + 1, base + PAIRS - 1) as pair:
                body(Tile(pair, 0), False, 2)
                body(Tile(pair, 1), False, 2)
            body(Tile(base + PAIRS - 1, 0), False, 1)
            body(Tile(base + PAIRS - 1, 1), False, 0)

        def slots(first):
            names = ("turn1", "drive", "scan", "readout", "y", "mid", "ln2", "turn2")
            at = (None, None, 0, 2, 3, 4, 5, KH + 1) if first else (0, 1, 1, 3, 3, 4, 5, KH + 1)
            return dict(zip(names, at))

        CASTS = {c: PIECES_H1 + c for c in range(KH // 2)} | {KH + 3: NWC - 1}
        CHECKS = {0: 1, 1: 2, 2: 5, 3: 6, KH: 3, KH + 1: 4, KH + 2: 7, KH + 3: 8, KH + 6: 9, KH + 7: 10}
        CHECK_ORDER = [0] + [CHECKS[c] for c in sorted(CHECKS)]
        assert sorted(CHECK_ORDER) == list(range(NWC)) and PIECES_H1 + len(CASTS) == NWC

        LAG = 3
        LN1_STATS, LN1_OUT = KH + 4, KH + 5
        HALVES = [(h, range(h * J // 2, (h + 1) * J // 2)) for h in range(2)]

        def mix_bank(t, layer, c):
            if isinstance(t.pair, int) and t.pair % PAIRS == 0 and t.par == 0 and layer == 0 and c < 2:
                return attn[c]
            return ffn[c % 4]

        def both_passes(eng, one_pass):
            one_pass(0)
            eng.wait_ge(verdict, 1)
            is_fine = eng.value_load(fine[0:1, 0:1], min_val=0, max_val=1)
            with eng.If(is_fine == 0):
                one_pass(1)

        @block.sync
        def _(sp):
            def rows_of(dram, exact, t, h):
                return dram[t.n - NT * exact].rearrange("(h j p) d -> h p j d", h=2, p=P)[h]

            def load_x(exact, t):
                for h, js in HALVES:
                    sp.dma_start(x_in[t.par][:, js[0]:js[-1] + 1, :], rows_of(x, exact, t, h)) \
                        .then_inc(x_loaded[t.par][h], 16)

            def load_w(n):
                if n >= STAGES + SPARE:
                    sp.wait_ge(w_checked, CHECK_ORDER.index(n - STAGES - SPARE) + 1)
                sp.dma_start(staged(n), w_all[:, n * WC:(n + 1) * WC]).then_inc(w_loaded[n], 16)

            def store(exact, t):
                for h, js in HALVES:
                    sp.wait_ge(out_ready, 2 * t.n + h + 1)
                    sp.dma_start(rows_of(out, exact, t, h), x_out[t.par][:, js[0]:js[-1] + 1, :]) \
                        .then_inc(stored[t.par], 16)

            def one_pass(exact):
                base = PAIRS * exact
                load_x(exact, Tile(base, 0))
                if not exact:
                    sp.dma_start(bw_sb[:, :, :, :], bw).then_inc(bw_loaded, 16)
                    sp.dma_start(a_sb[:, :], a_cols).then_inc(small_loaded, 16)
                    sp.dma_start(s_sb[:, :, :], s_cols).then_inc(small_loaded, 16)
                    sp.dma_start(rows_sb[:, :, :].rearrange("p a d -> p (a d)"),
                                 rows.partition_broadcast(P)).then_inc(small_loaded, 16)
                load_x(exact, Tile(base, 1))
                if exact:
                    sp.dma_start(w_f32[:, :], w_all[:, :]).then_inc(w_exact, 16)
                else:
                    for n in range(NWC):
                        load_w(n)

                def body(t, first, left):
                    if not first:
                        store(exact, t.prev())
                    if left == 2:
                        sp.wait_ge(x_used, 2 * t.n + 2)
                        load_x(exact, t.next().next())

                tiles(sp, exact, body)
                store(exact, Tile(base + PAIRS - 1, 1))
                for s in stored:
                    sp.wait_ge(s, 32 * (base + PAIRS))

            both_passes(sp, one_pass)

        @block.gpsimd
        def _(pool):
            pool.memset(ident[:, :], 0.0).then_inc(pool_step, 1)
            pool.memset(ones[:, :], 1.0).then_inc(ident_made, 1)
            pool.memset(eps[:, :], EPS).then_inc(pool_step, 1)
            pool.memset(minus_half[:, :], -0.5).then_inc(pool_step, 1)
            pool.wait_ge(pool_step, 3)
            pool.affine_select(out=ident[:, :], in_=ident[:, :], compare_op=ALU.not_equal, fill=1.0, base=0,
                               pattern=[[-1, P]], channel_multiplier=1).then_inc(ident_made, 1)

            def one_pass(exact):
                def rstd_of(kind, t):
                    for h, js in HALVES:
                        n = 2 * t.n + h + 1
                        half = slice(js[0], js[-1] + 1)
                        pool.wait_ge(var_done[kind], n)
                        pool.tensor_tensor(var_plus[:, kind, half], mean_var[:, kind, half, 1],
                                           eps[:, half], ALU.add).then_inc(var_eps[kind], 1)
                        pool.wait_ge(var_eps[kind], n)
                        pool.tensor_tensor(rstd[:, kind, half], var_plus[:, kind, half],
                                           minus_half[:, half], ALU.pow).then_inc(rstd_done[kind], 1)

                def body(t, first, left):
                    if not first:
                        rstd_of(3, t.prev())
                    if left:
                        rstd_of(1, t.next())
                        rstd_of(2, t.next())
                    if left == 2:
                        rstd_of(0, t.next().next())

                head = Tile(PAIRS * exact, 0)
                rstd_of(0, head)
                rstd_of(0, head.next())
                rstd_of(1, head)
                rstd_of(2, head)
                tiles(pool, exact, body)
                rstd_of(3, Tile(PAIRS * exact + PAIRS - 1, 1))

            both_passes(pool, one_pass)

        @block.tensor
        def _(pe):
            def one_pass(exact):
                def product(bank, w_at, op, k, start, stop):
                    if exact:
                        return pe.matmul(bank, w_f32[:, w_at:w_at + P], op[:, k, :], start=start, stop=stop)
                    w = w_f16[:, w_at:w_at + P]
                    pe.matmul(bank, w, hi(op, k), start=start, stop=False)
                    return pe.matmul(bank, w, lo(op, k), start=False, stop=stop)

                def turn(t, done, ready, banks=attn):
                    for h, js in HALVES:
                        pe.wait_ge(ready, 2 * t.n + h + 1)
                        for k in range(KD):
                            for j in js:
                                mm = pe.transpose(banks[k][:, j * P:(j + 1) * P],
                                                  normed[:, j, k * P:(k + 1) * P], ident[:, :])
                    mm.then_inc(done, 1)

                def drive(t, banks=attn):
                    pe.wait_ge(xT_ready, KD * t.n + KD)
                    for c in range(KD):
                        for k in range(KD):
                            mm = pe.matmul(banks[c][:, :], bw_sb[:, 0, k, c * P:(c + 1) * P], xT[:, k, :],
                                           start=(k == 0), stop=(k == KD - 1))
                        mm.then_inc(drive_done, 1)

                def readout(t):
                    pe.wait_ge(state_ready, KD * t.n + KD)
                    for j in range(J):
                        for k in range(KD):
                            mm = pe.matmul(attn[j // 2][:, j % 2 * D:(j % 2 + 1) * D],
                                           state[:, k, j * P:(j + 1) * P], bw_sb[:, 1, k, :],
                                           start=(k == 0), stop=(k == KD - 1))
                        if j % 2:
                            mm.then_inc(readout_done, 1)

                def up(t, c, head=False):
                    if c >= 2:
                        pe.wait_ge(h0_done, KH * t.n + c - 1)
                    elif not head:
                        pe.wait_ge(gelu_done, 2 * KH * t.n - 2 + 2 * c)
                    for half, at in enumerate((W1, W2)):
                        for k in range(KD):
                            if c == 0 and half == 0:
                                pe.wait_ge(x_split, KD * t.n + k + 1)
                            mm = product(ffn[2 * (c % 2) + half][:, :], at + k * HID + c * P, x_op, k,
                                         k == 0, k == KD - 1)
                    mm.then_inc(up_done, 1)

                def mix(t, layer, c):
                    n = layer * KH + c
                    if layer == 0 and c in (0, 2):
                        pe.wait_ge(h0_done, KH * t.n + KH - 1 + c // 2)
                    if n >= 4:
                        pe.wait_ge(gelu_done, 2 * KH * t.n + n - 3)
                    for k in range(KH):
                        if c == 0:
                            pe.wait_ge((h0_split, mix_split[0])[layer], KH * t.n + k + 1)
                        mm = mix_product(t, layer, c, k)
                    mm.then_inc(mix_done, 1)

                def mix_product(t, layer, c, k):
                    return product(mix_bank(t, layer, c)[:, :], (H1, H2)[layer] + k * HID + c * P, h_op[layer], k,
                                   k == 0, k == KH - 1)

                def head_up_and_mix(t):
                    if not exact:
                        pe.wait_ge(w_cast, PIECES_UP)
                    for c in range(KH):
                        up(t, c, head=True)
                        if not exact and c == LAG:
                            pe.wait_ge(w_cast, PIECES_H1)
                        if c >= LAG:
                            pe.wait_ge(h0_split, KH * t.n + c - LAG + 1)
                            mix_product(t, 0, 0, c - LAG)
                    for k in range(KH - LAG):
                        mix_product(t, 0, 1, k)
                    for k in range(KH - LAG, KH):
                        pe.wait_ge(h0_split, KH * t.n + k + 1)
                        for c in range(2):
                            mm = mix_product(t, 0, c, k)
                            if k == KH - 1:
                                mm.then_inc(mix_done, 1)

                def down_part(t, j, fresh):
                    if j == 0 and not fresh:
                        pe.wait_ge(z_ready, 2 * t.n)
                    bank = down[j // 2][:, j % 2 * D:(j % 2 + 1) * D]
                    for k in range(KH):
                        if j == 0:
                            pe.wait_ge(mix_split[1], KH * t.n + k + 1)
                        if exact:
                            mm = pe.matmul(bank, h_op[2][:, k, j * P:(j + 1) * P],
                                           w_f32[:, W3 + k * D:W3 + (k + 1) * D], start=(k == 0), stop=(k == KH - 1))
                        else:
                            w = w_f16[:, W3 + k * D:W3 + (k + 1) * D]
                            pe.matmul(bank, hi(h_op[2], k)[:, j * P:(j + 1) * P], w, start=(k == 0), stop=False)
                            mm = pe.matmul(bank, lo(h_op[2], k)[:, j * P:(j + 1) * P], w, start=False,
                                           stop=(k == KH - 1))
                    if j % 2:
                        mm.then_inc(down_done, 1)

                def body(t, first, left):
                    fresh = first and not exact
                    at = slots(first)
                    for c in range(2 * KH):
                        if fresh and c == KH:
                            pe.wait_ge(w_cast, PIECES_H2)
                        if not first or c >= 2:
                            mix(t, c // KH, c % KH)
                        if left:
                            if c == at["turn1"]:
                                turn(t.next(), turn1_done, ln1_out)
                            if c == at["drive"]:
                                drive(t.next())
                            if c == at["readout"]:
                                if first:
                                    pe.wait_ge(gelu_done, 2 * KH * t.n + 2)
                                readout(t.next())
                            if c == at["turn2"]:
                                turn(t.next(), turn2_done, ln2_out)
                    if fresh:
                        pe.wait_ge(w_cast, NWC)
                    for j in range(J):
                        if left:
                            up(t.next(), 2 * j)
                            up(t.next(), 2 * j + 1)
                        down_part(t, j, fresh)
                        if not exact and left == 0 and j == 0:
                            pe.wait_ge(bad_summed, 1)
                            pe.matmul(attn[0][0:1, 0:1], bad_sum[:, :], ones[:, :], start=True, stop=True) \
                                .then_inc(bad_total, 1)

                def keep_warm(n):
                    for _ in range(n):
                        pe.matmul(ffn[3][:, 0:P], ident[:, :], ident[:, :], start=True, stop=True)

                head = Tile(PAIRS * exact, 0)
                if exact:
                    pe.wait_ge(w_exact, 16)
                else:
                    pe.wait_ge(ident_made, 2)
                    keep_warm(10)
                turn(head, turn1_done, ln1_out)
                keep_warm(5)
                if not exact:
                    pe.wait_ge(bw_loaded, 16)
                drive(head)
                keep_warm(3)
                readout(head)
                turn(head.next(), turn1_done, ln1_out, banks=down)
                keep_warm(4)
                drive(head.next(), banks=down)
                keep_warm(6)
                turn(head, turn2_done, ln2_out)
                keep_warm(6)
                head_up_and_mix(head)
                tiles(pe, exact, body)

            both_passes(pe, one_pass)

        @block.scalar
        def _(act):
            def cast_w(n):
                act.wait_ge(w_loaded[n], 16)
                act.activation(w_f16[:, n * WC:(n + 1) * WC], staged(n), ACT.Copy).then_inc(w_cast, 1)

            def one_pass(exact):
                def turn1_copy(t, banks=attn):
                    act.wait_ge(turn1_done, t.n + 1)
                    for k in range(KD):
                        act.activation(xT[:, k, :], banks[k][:, :], ACT.Copy).then_inc(xT_ready, 1)

                def turn2_hi(t):
                    if exact:
                        return
                    act.wait_ge(turn2_done, t.n + 1)
                    for k in range(KD):
                        act.activation(hi(x_op, k), attn[k][:, :], ACT.Copy, scale=2.0 ** A_X).then_inc(x_hi, 1)

                def tanh(t, c):
                    act.wait_ge(up_done, KH * t.n + c + 1)
                    if c >= 2:
                        act.wait_ge(gate_done, KH * t.n + c - 1)
                    act.activation(tanh_u[c % 2][:, :], ffn[2 * (c % 2)][:, :], ACT.Tanh,
                                   scale=tanh_scale[:, c:c + 1]).then_inc(tanh_done, 1)

                def h0_hi_part(t, c):
                    if exact:
                        return
                    act.wait_ge(h0_done, KH * t.n + c + 1)
                    act.activation(hi(h_op[0], c), full[c % 2][:, :], ACT.Copy).then_inc(h0_hi, 1)

                def gelu(t, layer, c):
                    act.wait_ge(mix_done, 2 * KH * t.n + layer * KH + c + 1)
                    if c >= 2:
                        act.wait_ge(mix_split[layer], KH * t.n + c - 1)
                    act.activation(full[c % 2][:, :], mix_bank(t, layer, c)[:, :], ACT.Gelu,
                                   scale=mix_scale[:, layer, c:c + 1]).then_inc(gelu_done, 1)

                def up(t):
                    for c in range(KH):
                        tanh(t, c)
                        if c:
                            h0_hi_part(t, c - 1)
                    h0_hi_part(t, KH - 1)

                def body(t, first, left):
                    at = slots(first)
                    for c in range(2 * KH):
                        gelu(t, c // KH, c % KH)
                        if first and not exact and c in CASTS:
                            cast_w(CASTS[c])
                        if left:
                            if c == at["turn1"]:
                                turn1_copy(t.next())
                            if c == at["turn2"]:
                                turn2_hi(t.next())
                    if left:
                        up(t.next())

                head = Tile(PAIRS * exact, 0)
                turn1_copy(head)
                if not exact:
                    for n in range(PIECES_UP):
                        cast_w(n)
                turn1_copy(head.next(), banks=down)
                if not exact:
                    for n in range(PIECES_UP, PIECES_H1 - 1):
                        cast_w(n)
                turn2_hi(head)
                if not exact:
                    cast_w(PIECES_H1 - 1)
                    act.wait_ge(consts, 7)
                up(head)
                tiles(act, exact, body)

            both_passes(act, one_pass)

        @block.vector
        def _(dve):
            def check_w(n):
                dve.wait_ge(w_cast, n + 1)
                dve.scalar_tensor_tensor(out=staged(n), in0=staged(n), scalar=0.0,
                                         in1=w_f16[:, n * WC:(n + 1) * WC], op0=ALU.add, op1=ALU.not_equal,
                                         accum_out=bad[:, n:n + 1]).then_inc(w_checked, 1)

            def statistics(kind, t, half, src):
                h, js = half
                for j in js:
                    ins = dve.bn_stats(stats[:, kind, j, :], src[:, j, :])
                ins.then_inc(stats_done[kind], 1)
                dve.wait_ge(stats_done[kind], 2 * t.n + h + 1)
                dve.memset(scratch[:, :], 0.0)
                for j in js:
                    ins = dve.bn_aggr(mean_var[:, kind, j, :], stats[:, kind, j, :])
                ins.then_inc(var_done[kind], 1)

            def normalise(kind, t, half, dst, src):
                h, js = half
                dve.wait_ge(rstd_done[kind], 2 * t.n + h + 1)
                for j in js:
                    ins = dve.tensor_scalar(dst[:, j, :], src[:, j, :], mean_var[:, kind, j, 0:1],
                                            rstd[:, kind, j:j + 1], ALU.subtract, ALU.mult)
                return ins

            def one_pass(exact):
                def split(op, k, src, power, split_done, total=None):
                    if exact:
                        dve.tensor_scalar(op[:, k, :], src, 2.0 ** power, None, ALU.mult).then_inc(split_done, 1)
                    else:
                        dve.scalar_tensor_tensor(out=lo(op, k), in0=src, scalar=2.0 ** power, in1=hi(op, k),
                                                 op0=ALU.mult, op1=ALU.subtract,
                                                 accum_out=total).then_inc(split_done, 1)

                def check_range(t):
                    if not exact:
                        dve.wait_ge(mix_split[1], KH * t.n + KH)
                        dve.scalar_tensor_tensor(out=bad[:, NWC:], in0=lo_sum[:, :], scalar=0.0,
                                                 in1=bad[:, NWC:], op0=ALU.mult, op1=ALU.add).then_inc(range_checked, 1)

                def conclude():
                    dve.wait_ge(range_checked, NT)
                    dve.wait_ge(w_checked, NWC)
                    dve.tensor_reduce(bad_sum[:, :], bad[:, :], AX_X, ALU.add).then_inc(bad_summed, 1)
                    dve.wait_ge(bad_total, 1)
                    dve.tensor_scalar(fine[:, :], attn[0][0:1, 0:1], 0.0, None, ALU.is_equal).then_inc(verdict, 1)

                def ln1_stats(t):
                    for half in HALVES:
                        dve.wait_ge(x_loaded[t.par][half[0]], 16 * (t.pair + 1))
                        statistics(0, t, half, x_in[t.par])

                def ln1(t):
                    for half in HALVES:
                        normalise(0, t, half, normed, x_in[t.par]).then_inc(ln1_out, 1)

                def scan(t, banks=attn):
                    for c in range(KD):
                        dve.wait_ge(drive_done, KD * t.n + c + 1)
                        dve.tensor_tensor_scan(state[:, c, :], a_wide[:, c, :], banks[c][:, :], 0.0,
                                               ALU.mult, ALU.add).then_inc(state_ready, 1)

                def y_stage(t):
                    for h, js in HALVES:
                        dve.wait_ge(readout_done, 2 * t.n + h + 1)
                        dve.tensor_tensor(proj[:, 2 * h:2 * h + 2, :],
                                          attn[h][:, :].rearrange("p (a d) -> p a d", a=2),
                                          rows_sb[:, 0:1, :].to_broadcast([P, 2, D]), ALU.add) \
                            .then_inc(y_ready, 1)
                        dve.wait_ge(y_ready, 2 * t.n + h + 1)
                        statistics(1, t, (h, js), proj)

                def mid_stage(t):
                    for h, js in HALVES:
                        half = slice(js[0], js[-1] + 1)
                        normalise(1, t, (h, js), proj, proj).then_inc(y_normed, 1)
                        dve.wait_ge(y_normed, 2 * t.n + h + 1)
                        dve.tensor_tensor(x_mid[t.par][:, half, :], x_in[t.par][:, half, :], proj[:, half, :],
                                          ALU.add).then_inc(x_used, 1)
                        dve.wait_ge(x_used, 2 * t.n + h + 1)
                        statistics(2, t, (h, js), x_mid[t.par])

                def ln2(t):
                    for half in HALVES:
                        normalise(2, t, half, normed, x_mid[t.par]).then_inc(ln2_out, 1)

                def x_lo(t):
                    dve.wait_ge(turn2_done, t.n + 1)
                    for k in range(KD):
                        if not exact:
                            dve.wait_ge(x_hi, KD * t.n + k + 1)
                        split(x_op, k, attn[k][:, :], A_X, x_split)

                def h0(t, c):
                    dve.wait_ge(tanh_done, KH * t.n + c + 1)
                    dve.scalar_tensor_tensor(out=gate[c % 2][:, :], in0=tanh_u[c % 2][:, :], scalar=1.0,
                                             in1=ffn[2 * (c % 2)][:, :], op0=ALU.add, op1=ALU.mult) \
                        .then_inc(gate_done, 1)
                    dve.wait_ge(gate_done, KH * t.n + c + 1)
                    dve.scalar_tensor_tensor(out=full[c % 2][:, :], in0=ffn[2 * (c % 2) + 1][:, :],
                                             scalar=gate_scale[:, c:c + 1], in1=gate[c % 2][:, :],
                                             op0=ALU.mult, op1=ALU.mult).then_inc(h0_done, 1)

                def h0_lo(t, c):
                    if exact:
                        dve.wait_ge(h0_done, KH * t.n + c + 1)
                    else:
                        dve.wait_ge(h0_hi, KH * t.n + c + 1)
                    split(h_op[0], c, full[c % 2][:, :], 0, h0_split, lo_sum[:, c:c + 1])

                def gelu_split(t, layer, c):
                    power = (A_H1, A_H2)[layer]
                    n = 2 * KH * t.n + layer * KH + c + 1
                    dve.wait_ge(gelu_done, n)
                    if not exact:
                        dve.tensor_scalar(hi(h_op[1 + layer], c), full[c % 2][:, :], 2.0 ** power, None,
                                          ALU.mult).then_inc(g_hi, 1)
                        dve.wait_ge(g_hi, n)
                    at = (1 + layer) * KH + c
                    split(h_op[1 + layer], c, full[c % 2][:, :], power, mix_split[layer], lo_sum[:, at:at + 1])

                def z_stage(t, halves=HALVES):
                    for h, js in halves:
                        dve.wait_ge(down_done, 2 * t.n + h + 1)
                        dve.tensor_tensor(proj[:, 2 * h:2 * h + 2, :],
                                          down[h][:, :].rearrange("p (a d) -> p a d", a=2),
                                          s3_row[:, :, :].to_broadcast([P, 2, D]), ALU.mult) \
                            .then_inc(z_ready, 1)
                        dve.wait_ge(z_ready, 2 * t.n + h + 1)
                        statistics(3, t, (h, js), proj)

                def out_stage(t, halves=HALVES):
                    for h, js in halves:
                        half = slice(js[0], js[-1] + 1)
                        n = 2 * t.n + h + 1
                        normalise(3, t, (h, js), proj, proj).then_inc(z_normed, 1)
                        dve.wait_ge(z_normed, n)
                        if not (isinstance(t.pair, int) and t.pair == 0):
                            dve.wait_ge(stored[t.par], 32 * t.pair)
                        dve.tensor_tensor(x_out[t.par][:, half, :], x_mid[t.par][:, half, :], proj[:, half, :],
                                          ALU.add).then_inc(out_ready, 1)

                def up(t, head=False):
                    for c in range(KH):
                        h0(t, c)
                        if c:
                            h0_lo(t, c - 1)
                        elif not head:
                            check_range(t.prev())
                    h0_lo(t, KH - 1)

                def body(t, first, left):
                    at = slots(first)
                    for c in range(2 * KH):
                        if first and not exact and c in CHECKS:
                            check_w(CHECKS[c])
                        gelu_split(t, c // KH, c % KH)
                        if not first:
                            if c == 0:
                                z_stage(t.prev())
                            if c == 1:
                                out_stage(t.prev())
                        if left:
                            if c == at["scan"]:
                                scan(t.next(), banks=down if first else attn)
                            if c == at["y"]:
                                y_stage(t.next())
                            if c == at["mid"]:
                                mid_stage(t.next())
                            if c == at["ln2"]:
                                ln2(t.next())
                            if c == at["turn2"]:
                                x_lo(t.next())
                        if left == 2:
                            if c == LN1_STATS:
                                ln1_stats(t.next().next())
                            if c == LN1_OUT:
                                ln1(t.next().next())
                    if left:
                        up(t.next())
                    else:
                        check_range(t)
                        if not exact:
                            conclude()
                        for half in HALVES:
                            z_stage(t, [half])
                            out_stage(t, [half])

                head = Tile(PAIRS * exact, 0)
                if not exact:
                    dve.memset(a_wide[:, :, :], 0.0).then_inc(zeroed, 1)
                ln1_stats(head)
                ln1(head)
                if not exact:
                    dve.wait_ge(small_loaded, 48)
                    dve.wait_ge(zeroed, 1)
                    for c in range(KD):
                        dve.tensor_scalar(a_wide[:, c, :], a_wide[:, c, :], a_sb[:, c:c + 1], None, ALU.add) \
                            .then_inc(consts, 1)
                    dve.tensor_scalar(s3_row[:, 0, :], rows_sb[:, 1, :], 2.0 ** -A_H2, None, ALU.mult)
                    dve.tensor_scalar(tanh_scale[:, :], s_sb[:, 0, :], 2.0 ** -(A_X + 1), None, ALU.mult) \
                        .then_inc(consts, 1)
                    dve.tensor_tensor(ss[:, :], s_sb[:, 0, :], s_sb[:, 1, :], ALU.mult).then_inc(consts, 1)
                    dve.tensor_scalar(mix_scale[:, 0, :], s_sb[:, 2, :], 2.0 ** -A_H0, None, ALU.mult) \
                        .then_inc(consts, 1)
                    dve.tensor_scalar(mix_scale[:, 1, :], s_sb[:, 3, :], 2.0 ** -A_H1, None, ALU.mult) \
                        .then_inc(consts, 1)
                    dve.wait_ge(consts, 6)
                    dve.tensor_scalar(gate_scale[:, :], ss[:, :], 2.0 ** (A_H0 - 2 * A_X - 1), None, ALU.mult) \
                        .then_inc(consts, 1)
                    dve.memset(bad[:, :], 0.0).then_inc(consts, 1)
                    dve.wait_ge(consts, 8)
                ln1_stats(head.next())
                scan(head)
                dve.wait_ge(turn1_done, head.n + 1)
                ln1(head.next())
                y_stage(head)
                mid_stage(head)
                dve.wait_ge(turn1_done, head.n + 2)
                ln2(head)
                x_lo(head)
                if not exact:
                    check_w(0)
                up(head, head=True)
                tiles(dve, exact, body)

            both_passes(dve, one_pass)


def _packed(w):
    import numpy as np
    n_out, n_in = w.shape
    return np.ascontiguousarray(w.T.reshape(n_in // P, P, n_out).transpose(1, 0, 2)).reshape(P, -1)


def kernel(L0_attn_x, L0_attn_A, L0_attn_B, L0_attn_W, L0_attn_b, L0_ffn_w1_w, L0_ffn_w1_s, L0_ffn_w2_w,
           L0_ffn_w2_s, L0_ffn_h1_w, L0_ffn_h1_s, L0_ffn_h2_w, L0_ffn_h2_s, L0_ffn_w3_w, L0_ffn_w3_s):
    import numpy as np
    import concourse.bacc as bacc
    from concourse.bass_utils import run_bass_kernel_spmd

    def columns(v):
        return np.asarray(v).reshape(-1, P).T

    D = L0_attn_x.shape[2]
    arrays = {
        "x_dram": np.ascontiguousarray(L0_attn_x),
        "bw_dram": np.ascontiguousarray(np.stack(
            [_packed(np.asarray(m)).reshape(P, D // P, D) for m in (L0_attn_B, L0_attn_W)], axis=1)),
        "a_dram": np.ascontiguousarray(columns(L0_attn_A)),
        "w_dram": np.ascontiguousarray(np.concatenate(
            [_packed(np.asarray(w)) for w in (L0_ffn_w1_w, L0_ffn_w2_w, L0_ffn_h1_w, L0_ffn_h2_w, L0_ffn_w3_w)],
            axis=1)),
        "s_dram": np.ascontiguousarray(np.stack(
            [columns(s) for s in (L0_ffn_w1_s, L0_ffn_w2_s, L0_ffn_h1_s, L0_ffn_h2_s)], axis=1)),
        "rows_dram": np.ascontiguousarray(np.concatenate([np.asarray(L0_attn_b), np.asarray(L0_ffn_w3_s)])),
    }
    nc = bacc.Bacc("TRN2", target_bir_lowering=False, num_devices=1)
    args = [nc.dram_tensor(name, a.shape, mybir.dt.from_np(a.dtype), kind="ExternalInput").ap()
            for name, a in arrays.items()]
    out = nc.dram_tensor("out_dram", L0_attn_x.shape, F32, kind="ExternalOutput").ap()
    ssm_ffn_kernel(nc, *args, out)
    result = run_bass_kernel_spmd(nc, [arrays], core_ids=[0])
    return result.results[0]["out_dram"]
```
